# Optimizing a Trainium2 kernel written in Bass

```python
import numpy as np
import jax
import jax.numpy as jnp

def _softmax(x, axis=-1):
    return jax.nn.softmax(x, axis=axis)

def _gelu(x):
    return jax.nn.gelu(x, approximate=True)

def _silu(x):
    return jax.nn.silu(x)

def _sigmoid(x):
    return jax.nn.sigmoid(x)

def _layernorm(x, axis=-1, eps=1e-05):
    m = jnp.mean(x, axis=axis, keepdims=True)
    v = jnp.var(x, axis=axis, keepdims=True)
    return (x - m) / jnp.sqrt(v + eps)

def _scatter_add(tgt, idx, src, axis=0):
    return tgt.at[idx].add(src)

def _segment_sum(src, seg, n):
    return jax.ops.segment_sum(src, seg, n)
kernel_name = 'mk_perceiver_d1_seqx_r8_eab2a7'

def setup_inputs(seed: int=0):
    np.random.seed(seed)
    _w = jnp.asarray

    def _rec_inputs():
        import jax
        import jax.numpy as jnp
        _rk = jax.random.key(seed)
        x = -7.109e-05 + 0.9999 * jax.random.normal(jax.random.fold_in(_rk, 1), (1, 128, 512), jnp.float32)
        _lenS = 128 - jax.random.randint(jax.random.fold_in(_rk, 7), (1,), 0, max(1, 128 // 4) + 1, jnp.int32)
        _lenS2 = 2048 - jax.random.randint(jax.random.fold_in(_rk, 8), (1,), 0, max(1, 2048 // 4) + 1, jnp.int32)
        _ctx_4096P = jax.random.normal(jax.random.fold_in(_rk, 11), (1, 16, 512), jnp.float32)
        _ctx_4096c = jax.random.dirichlet(jax.random.fold_in(_rk, 511), 0.3 * jnp.ones((16,), jnp.float32), (1, 2048))
        _ctx_4096t = jnp.einsum('bsk,bkd->bsd', _ctx_4096c, _ctx_4096P)
        _ctx_4096t = _ctx_4096t * jax.lax.rsqrt(jnp.mean(jnp.square(_ctx_4096t)) + 1e-12) * 0.953939
        ctx_4096 = -0.00010331 + 0.999899 * (_ctx_4096t + 0.3 * jax.random.normal(jax.random.fold_in(_rk, 611), (1, 2048, 512), jnp.float32))
        return (x, ctx_4096)
    x, ctx_4096 = _rec_inputs()

    def _L0_xattn_setup():
        import jax, jax.numpy as jnp
        import numpy as np
        key = jax.random.key(seed)
        k1, k2 = jax.random.split(key)
        B, Lq, Lk, D = (16, 128, 256, 512)
        query = jax.random.normal(k1, (B, Lq, D), dtype=jnp.float32)
        key_t = jax.random.normal(k2, (B, Lk, D), dtype=jnp.float32)
        return {'query': query, 'key': key_t}
    _L0_xattn_all = _L0_xattn_setup()
    _L0_xattn_in = {k: v for k, v in _L0_xattn_all.items() if k in ()}
    del _L0_xattn_all

    def _L0_attn_setup():
        import jax, jax.numpy as jnp
        import numpy as np
        B, S, EMB = (2, 256, 512)
        NHEADS, KVHEADS, HEAD_D = (32, 8, 128)
        SPLITS = (NHEADS * HEAD_D, KVHEADS * HEAD_D, KVHEADS * HEAD_D)
        key = jax.random.key(seed)
        k1, k2, k3 = jax.random.split(key, 3)
        q = jax.random.normal(k1, (B, S, EMB), dtype=jnp.float32)
        w_qkv = jax.random.normal(k2, (sum(SPLITS), EMB), dtype=jnp.float32) * 0.02
        w_dense = jax.random.normal(k3, (EMB, NHEADS * HEAD_D), dtype=jnp.float32) * 0.02
        return {'q': q, 'w_qkv': w_qkv, 'w_dense': w_dense}
    _L0_attn_all = _L0_attn_setup()
    _L0_attn_in = {k: v for k, v in _L0_attn_all.items() if k in ('w_qkv', 'w_dense')}
    del _L0_attn_all

    def _L0_ffn_setup():
        import jax, jax.numpy as jnp
        import numpy as np
        HD, M = (512, 1792)
        key = jax.random.key(seed)
        k_x, k_g, k_u, k_d = jax.random.split(key, 4)
        scale = 1.0 / np.sqrt(HD)
        x = jax.random.normal(k_x, (4, 256, HD), dtype=jnp.float16)
        W_gate = jax.random.normal(k_g, (M, HD), dtype=jnp.float16) * jnp.float16(scale)
        W_up = jax.random.normal(k_u, (M, HD), dtype=jnp.float16) * jnp.float16(scale)
        W_down = jax.random.normal(k_d, (HD, M), dtype=jnp.float16) * jnp.float16(1.0 / np.sqrt(M))
        return {'x': x, 'W_gate': W_gate, 'W_up': W_up, 'W_down': W_down}
    _L0_ffn_all = _L0_ffn_setup()
    _L0_ffn_in = {k: v for k, v in _L0_ffn_all.items() if k in ('W_gate', 'W_up', 'W_down')}
    del _L0_ffn_all
    return {'x': x, 'ctx_4096': ctx_4096, 'L0_attn_w_qkv': _L0_attn_in['w_qkv'], 'L0_attn_w_dense': _L0_attn_in['w_dense'], 'L0_ffn_W_gate': _L0_ffn_in['W_gate'], 'L0_ffn_W_up': _L0_ffn_in['W_up'], 'L0_ffn_W_down': _L0_ffn_in['W_down']}

def reference(x, ctx_4096, L0_attn_w_qkv, L0_attn_w_dense, L0_ffn_W_gate, L0_ffn_W_up, L0_ffn_W_down):
    import jax
    import jax.numpy as jnp

    def _L0_xattn_ref(query, key):
        import jax, jax.numpy as jnp
        import numpy as np
        a = jnp.einsum('bqd,bkd->bqk', query, key)
        e = jax.nn.softmax(a, axis=-1)
        c = jnp.einsum('bqk,bkd->bqd', e, key)
        return c

    def _L0_attn_ref(q, w_qkv, w_dense):
        import jax, jax.numpy as jnp
        import numpy as np
        B, S, EMB = (2, 256, 512)
        NHEADS, KVHEADS, HEAD_D = (32, 8, 128)
        SPLITS = (NHEADS * HEAD_D, KVHEADS * HEAD_D, KVHEADS * HEAD_D)
        Bq, Sq, _ = q.shape
        qkv = q @ w_qkv.T
        qs, ks, vs = jnp.split(qkv, np.cumsum(SPLITS)[:-1], axis=-1)
        G = NHEADS // KVHEADS
        qh = qs.reshape(Bq, Sq, KVHEADS, G, HEAD_D)
        kh = ks.reshape(Bq, Sq, KVHEADS, HEAD_D)
        vh = vs.reshape(Bq, Sq, KVHEADS, HEAD_D)
        scale = 1.0 / jnp.sqrt(jnp.float32(HEAD_D))
        scores = jnp.einsum('bskgd,btkd->bkgst', qh, kh) * scale
        causal = jnp.tril(jnp.ones((Sq, Sq), dtype=bool))
        scores = jnp.where(causal, scores, jnp.finfo(scores.dtype).min)
        probs = jax.nn.softmax(scores, axis=-1)
        attn = jnp.einsum('bkgst,btkd->bskgd', probs, vh)
        attn = attn.reshape(Bq, Sq, NHEADS * HEAD_D)
        return attn @ w_dense.T

    def _L0_ffn_ref(x, W_gate, W_up, W_down):
        import jax, jax.numpy as jnp
        import numpy as np
        HD, M = (512, 1792)
        gate = jnp.einsum('bsh,mh->bsm', x, W_gate)
        up = jnp.einsum('bsh,mh->bsm', x, W_up)
        h = jax.nn.silu(gate) * up
        out = jnp.einsum('bsm,hm->bsh', h, W_down)
        return out
    x = x + _L0_xattn_ref(_layernorm(x, axis=-1), ctx_4096)
    x = x + _L0_attn_ref(_layernorm(x, axis=-1), L0_attn_w_qkv, L0_attn_w_dense)
    x = x + _L0_ffn_ref(_layernorm(x, axis=-1), L0_ffn_W_gate, L0_ffn_W_up, L0_ffn_W_down)
    return x

_drawn_inputs = setup_inputs


def setup_inputs(seed=0):
    import zlib

    import numpy as np

    out = dict(_drawn_inputs(seed))
    spreads = {}
    factors = {}
    for name, (base, spread) in spreads.items():
        noise = np.random.default_rng([zlib.crc32(name.encode()), seed]).standard_normal(out[name].shape)
        drawn = base * np.exp(spread * noise) if base else spread * noise
        out[name] = jnp.asarray(drawn.astype(out[name].dtype))
    for name, factor in factors.items():
        out[name] = (out[name] * factor).astype(out[name].dtype)
    return out
```

```python
from contextlib import ExitStack

import concourse.bass as bass
from concourse import mybir

ALU = mybir.AluOpType
ACT = mybir.ActivationFunctionType
AX_X = mybir.AxisListType.X
F32 = mybir.dt.float32
F32R = mybir.dt.float32r
F16 = mybir.dt.float16
BF16 = mybir.dt.bfloat16
U32 = mybir.dt.uint32

P = 128
TB = 4
RAW_SLOTS = 6
WT_SLOTS = 14
TP_BANKS = 3
ATT_SLOTS = 3
LEAD = 3
EPS = 1e-5
MASKED = -1e30


def plan_blocks(n_ctx, n_kv, n_q):
    blocks = [("ctx", i) for i in range(n_ctx)]
    blocks += [("k", i) for i in range(n_kv)] + [("v", i) for i in range(n_kv)]
    blocks += [("q", 0), ("q", 1)]
    for g in range(2, n_q):
        blocks += [("q", g), ("dense", g - 2)]
    return blocks + [("dense", n_q - 2), ("dense", n_q - 1)]


def perceiver_layer_kernel(nc: bass.Bass, x, ctx_in, w_qkv, w_dense, w_gate, w_up, w_down, out):
    _, S, D = x.shape
    SK = ctx_in.shape[1]
    HD = w_dense.shape[1]
    M = w_gate.shape[0]
    DH = 128
    KVD = (w_qkv.shape[0] - HD) // 2
    KVH = KVD // DH
    G = HD // KVD
    BW = TB * P
    assert S == P and D == BW and G == TB and SK % BW == 0 and M % (4 * 64) == 0
    SCALE = float(DH) ** -0.5
    NCTX, NKV, NQ = SK // BW, KVD // BW, HD // BW

    BLOCKS = plan_blocks(NCTX, NKV, NQ)
    NB = len(BLOCKS)
    NU = NB * TB
    last_unit = {k: b * TB + TB - 1 for b, k in enumerate(BLOCKS)}

    PC_IN = D // 4 // 64
    PC_DN = M // 4 // 64
    JG, JD = M // 32, D // 32
    NF = -(-PC_DN // 2)

    with ExitStack() as ctx:
        def sb(name, shape, dt=F32):
            return ctx.enter_context(nc.sbuf_tensor(name, shape, dt))

        def sem(name):
            return ctx.enter_context(nc.semaphore(name))

        raw = sb("raw", [P, RAW_SLOTS, TB, BW])
        wt_hi = sb("wt_hi", [P, WT_SLOTS, BW], F32R)
        wt_lo = sb("wt_lo", [P, WT_SLOTS, BW], F32R)
        ffn_wt = sb("ffn_wt", [P, 3, M * 2])
        x_sb = sb("x_sb", [P, D])
        x1_sb = sb("x1_sb", [P, D])
        xn_sb = sb("xn_sb", [P, D])
        xT_hi = sb("xT_hi", [P, TB, P], F32R)
        xT_lo = sb("xT_lo", [P, TB, P], F32R)
        kT_hi = sb("kT_hi", [P, KVH, P], F32R)
        kT_lo = sb("kT_lo", [P, KVH, P], F32R)
        v_hi = sb("v_hi", [P, KVH, P], F32R)
        v_lo = sb("v_lo", [P, KVH, P], F32R)
        qk_sb = sb("qk_sb", [P, BW])
        qT_hi = sb("qT_hi", [P, G * P], F32R)
        qT_lo = sb("qT_lo", [P, G * P], F32R)
        p_sb = sb("p_sb", [P, G, P])
        pn_sb = sb("pn_sb", [P, G, P])
        pT_hi = sb("pT_hi", [P, G * P], F32R)
        pT_lo = sb("pT_lo", [P, G * P], F32R)
        aT_hi = sb("aT_hi", [P, ATT_SLOTS, G, P], F32R)
        aT_lo = sb("aT_lo", [P, ATT_SLOTS, G, P], F32R)
        ident = sb("ident", [P, P])
        ident_b = sb("ident_b", [P, P], BF16)
        mask = sb("mask", [P, G, P], BF16)
        stats = sb("stats", [P, 3, 6])
        mv = sb("mv", [P, 3, 2])
        rstd = sb("rstd", [P, 3])
        var_eps = sb("var_eps", [P, 3])
        minus_half = sb("minus_half", [P, 1])
        x_max = sb("x_max", [P, NCTX])
        x_negmax = sb("x_negmax", [P, 2])
        x_sum = sb("x_sum", [P, NCTX])
        x_tot = sb("x_tot", [P, 2])
        s_max = sb("s_max", [P, NQ, G])
        s_negmax = sb("s_negmax", [P, NQ, G])
        s_sum = sb("s_sum", [P, NQ, G])
        s_inv = sb("s_inv", [P, NQ, G])

        flat = ffn_wt[:].rearrange("p a b -> p (a b)")
        xp_sb = flat[:, 0:SK].rearrange("p (b n) -> p b n", b=NCTX)
        xpT_sb = flat[:, SK:2 * SK].rearrange("p (b n) -> p b n", b=NCTX)
        GROW = M * 2
        area = raw[:].rearrange("p s t n -> p (s t n)")
        down_raw = area[:, 0:GROW]
        taken = [GROW]

        def carve(n, dt=F32):
            words = n if dt == F32 else n // 2
            v = area[:, taken[0]:taken[0] + words]
            taken[0] += words
            return v if dt == F32 else v.bitcast(dt)

        x2_sb = carve(D)
        x3T_hi = carve(TB * P, F16).rearrange("p (c t) -> p c t", c=TB)
        x3T_lo = carve(TB * P, F16).rearrange("p (c t) -> p c t", c=TB)
        silu_sb = [carve(BW) for _ in range(NF)]
        h_sb = [carve(BW) for _ in range(NF)]
        hT_rest = silu_sb
        hT_hi = [carve(BW, BF16) for _ in range(NF)]
        hT_mid = [carve(BW, BF16) for _ in range(NF)]
        hT_lo = [carve(BW, BF16) for _ in range(NF)]
        out_sb = carve(D)

        bank = [ctx.enter_context(nc.psum_tensor(f"bank{i}", [P, BW], F32)) for i in range(8)]
        tp = bank[0:TP_BANKS]
        x_scores = bank[3:3 + NCTX]
        x_out = bank[7]
        proj, scores, xpose, att_out, dense = bank[3:8]

        raw_landed = [sem(f"raw_landed{i}") for i in range(RAW_SLOTS)]
        x_landed = sem("x_landed")
        ffn_landed = [sem(f"ffn_landed{i}") for i in range(3)]
        out_stored = sem("out_stored")
        consts_ready = sem("consts_ready")
        unit_transposed = sem("unit_transposed")
        hi_ready = sem("hi_ready")
        lo_ready = sem("lo_ready")
        unit_used = sem("unit_used")
        var_ready = sem("var_ready")
        rstd_ready = sem("rstd_ready")
        norm_ready = sem("norm_ready")
        xpose_ready = sem("xpose_ready")
        xpose_hi_ready = sem("xpose_hi_ready")
        xpose_lo_ready = sem("xpose_lo_ready")
        x_negmax_ready = sem("x_negmax_ready")
        x_exp_ready = sem("x_exp_ready")
        x_pT_ready = sem("x_pT_ready")
        x_pT_copied = sem("x_pT_copied")
        x_pv_done = sem("x_pv_done")
        qk_copied = sem("qk_copied")
        v_hi_ready = sem("v_hi_ready")
        v_lo_ready = sem("v_lo_ready")
        scored = sem("scored")
        negmax_ready = sem("negmax_ready")
        exp_ready = sem("exp_ready")
        inv_ready = sem("inv_ready")
        probs_ready = sem("probs_ready")
        pT_ready = sem("pT_ready")
        pT_hi_ready = sem("pT_hi_ready")
        pT_lo_ready = sem("pT_lo_ready")
        att_ready = sem("att_ready")
        aT_hi_ready = sem("aT_hi_ready")
        aT_lo_ready = sem("aT_lo_ready")
        dve_done = sem("dve_done")
        ffn_wt_ready = [sem(f"ffn_wt_ready{i}") for i in range(3)]
        gate_ready = sem("gate_ready")
        up_ready = sem("up_ready")
        silu_ready = sem("silu_ready")
        h_ready = sem("h_ready")
        hT_ready = sem("hT_ready")
        hT_hi_ready = sem("hT_hi_ready")
        rest_ready = sem("rest_ready")
        hT_mid_ready = sem("hT_mid_ready")
        hT_lo_ready = sem("hT_lo_ready")
        down_done = sem("down_done")
        result_ready = sem("result_ready")

        def block_src(kind, i):
            if kind == "dense":
                return w_dense[:, i * BW:(i + 1) * BW].rearrange("(t p) n -> p t n", p=P)
            rows = {"ctx": ctx_in[0], "q": w_qkv[0:HD], "k": w_qkv[HD:HD + KVD], "v": w_qkv[HD + KVD:]}[kind]
            return rows[i * BW:(i + 1) * BW].rearrange("(t p) n -> p t n", p=P)

        ffn_raw = [ffn_wt[:, 1, :], ffn_wt[:, 2, :], down_raw]
        ffn_dram = [w_gate, w_up, w_down]
        ffn_pc = [PC_IN, PC_IN, PC_DN]
        ffn_j = [JG, JG, JD]
        ffn_step_j = [512 // (32 * pc) for pc in ffn_pc]
        ffn_ops = [j // s for j, s in zip(ffn_j, ffn_step_j)]

        def ffn_view(w, part):
            return ffn_wt[:, w, :].bitcast(F16).rearrange("p (c n h) -> p c n h", c=ffn_pc[w], h=2)[part]

        PROJ = [k for k in BLOCKS if k[0] in "kvq"]
        QK = [k for k in PROJ if k[0] != "v"]
        COPY, XPOSE, SCORE, PROBS, VALUES = 1, 2, 4, 7, 9
        X_AHEAD = NCTX * TB + LEAD + 2
        KV_AHEAD = RAW_SLOTS * TB
        PV_AHEAD = KV_AHEAD + TP_BANKS
        STEPS = range(NCTX * TB, NU)
        N_LN = 2

        def ended(step, lag):
            return [k for k in PROJ if last_unit[k] + lag == step]

        ffn_at = {}
        for n in range(ffn_ops[0]):
            ffn_at[TB * 10 + 3 * n] = (0, n)
        for n in range(ffn_ops[1]):
            ffn_at[TB * 15 + 2 + 3 * n] = (1, n)
        GATE_AT, UP_AT = 12, 15

        groups = [min(2, PC_DN - 2 * f) for f in range(NF)]
        gate_bank = [bank[i] for i in (0, 2, 4, 0)]
        up_bank = [bank[i] for i in (1, 3, 6, 1)]
        hT_bank = [bank[i] for i in (5, 2, 5, 2)]

        block = ctx.enter_context(nc.Block())

        @block.sync
        def _(sp):
            sp.dma_start(x_sb[:], x[0]).then_inc(x_landed, 16)

            def load_ffn(w):
                pc = ffn_pc[w]
                dst = ffn_raw[w].bitcast(F16).rearrange("p (j d) -> p j d", j=ffn_j[w])
                for i in range(4):
                    src = ffn_dram[w][:, i * pc * 64:(i + 1) * pc * 64].rearrange("(j b) d -> b j d", b=32)
                    sp.dma_start(dst[32 * i:32 * i + 32], src).then_inc(ffn_landed[w], 16)

            for b, (kind, i) in enumerate(BLOCKS):
                old = b - RAW_SLOTS
                if old >= 0 and BLOCKS[old][0] == "ctx":
                    sp.wait_ge(x_pv_done, old + 1)
                elif old >= 0:
                    sp.wait_ge(unit_transposed, TB * (old + 1))
                if b == GATE_AT:
                    sp.wait_ge(x_pv_done, NCTX)
                    load_ffn(0)
                if b == UP_AT:
                    load_ffn(1)
                sp.dma_start(raw[:, b % RAW_SLOTS], block_src(kind, i)).then_inc(raw_landed[b % RAW_SLOTS], 16)
            sp.wait_ge(unit_transposed, TB * (NB - RAW_SLOTS + 2))
            load_ffn(2)
            sp.wait_ge(result_ready, 1)
            sp.dma_start(out[0], out_sb).then_inc(out_stored, 16)
            sp.wait_ge(out_stored, 16)

        CONSTS = 7

        @block.gpsimd
        def _(pool):
            def inverse_root(k):
                pool.wait_ge(var_ready, k + 1)
                nc.gpsimd.tensor_tensor(rstd[:, k:k + 1], var_eps[:, k:k + 1], minus_half[:],
                                        ALU.pow).then_inc(rstd_ready, 1)

            nc.gpsimd.memset(minus_half[:], -0.5).then_inc(consts_ready, 1)
            nc.gpsimd.memset(ident[:], 0.0).then_inc(consts_ready, 1)
            nc.gpsimd.memset(ident_b[:], 0.0).then_inc(consts_ready, 1)
            nc.gpsimd.memset(mask[:], 0.0).then_inc(consts_ready, 1)
            pool.wait_ge(consts_ready, 4)
            for m in (ident, ident_b):
                nc.gpsimd.affine_select(out=m[:], in_=m[:], compare_op=ALU.not_equal, fill=1.0, base=0,
                                        pattern=[[-1, P]], channel_multiplier=1).then_inc(consts_ready, 1)
            nc.gpsimd.affine_select(out=mask[:], in_=mask[:], compare_op=ALU.is_ge, fill=MASKED, base=0,
                                    pattern=[[0, G], [-1, P]], channel_multiplier=1).then_inc(consts_ready, 1)
            inverse_root(0)
            inverse_root(1)
            for g in range(NQ):
                pool.wait_ge(inv_ready, g + 1)
                if g >= 1:
                    pool.wait_ge(pT_ready, g)
                nc.gpsimd.tensor_tensor(pn_sb[:], p_sb[:], s_inv[:, g, :].unsqueeze(2).to_broadcast([P, G, P]),
                                        ALU.mult).then_inc(probs_ready, 1)
            inverse_root(2)

        @block.tensor
        def _(pe):
            done = [0]

            def transposes_to(n):
                for u in range(done[0], min(n, NU)):
                    b, c = divmod(u, TB)
                    if c == 0:
                        pe.wait_ge(raw_landed[b % RAW_SLOTS], 16 * (b // RAW_SLOTS + 1))
                    if u >= TP_BANKS:
                        pe.wait_ge(lo_ready, u - TP_BANKS + 1)
                    for t in range(TB):
                        last = nc.tensor.transpose(tp[u % TP_BANKS][:, t * P:(t + 1) * P],
                                                   raw[:, b % RAW_SLOTS, t, c * P:(c + 1) * P], ident[:])
                    last.then_inc(unit_transposed, 1)
                done[0] = max(done[0], min(n, NU))

            def transpose4(dst, tile_of, signal):
                for t in range(TB):
                    last = nc.tensor.transpose(dst[:, t * P:(t + 1) * P], tile_of(t), ident[:])
                last.then_inc(signal, 1)

            def product(u):
                b, c = divmod(u, TB)
                kind, i = BLOCKS[b]
                first, final = c == 0, c == TB - 1
                if kind == "dense":
                    hi, lo, dst = aT_hi[:, i % ATT_SLOTS, c, :], aT_lo[:, i % ATT_SLOTS, c, :], dense
                    first, final = first and i == 0, final and i == NQ - 1
                    if c == 0:
                        pe.wait_ge(aT_lo_ready, i + 1)
                elif kind == "ctx":
                    hi, lo, dst = xT_hi[:, c, :], xT_lo[:, c, :], x_scores[i]
                    if u == 0:
                        pe.wait_ge(xpose_lo_ready, 1)
                else:
                    hi, lo, dst = xT_hi[:, c, :], xT_lo[:, c, :], proj
                    n = PROJ.index((kind, i))
                    if c == 0 and n == 0:
                        pe.wait_ge(xpose_lo_ready, 2)
                    elif c == 0 and PROJ[n - 1][0] == "v":
                        pe.wait_ge(v_lo_ready, PROJ[n - 1][1] + 1)
                    elif c == 0:
                        pe.wait_ge(qk_copied, QK.index(PROJ[n - 1]) + 1)
                pe.wait_ge(lo_ready, u + 1)
                w_hi, w_lo = wt_hi[:, u % WT_SLOTS, :], wt_lo[:, u % WT_SLOTS, :]
                nc.tensor.matmul(dst[:], hi, w_hi, start=first, stop=False)
                nc.tensor.matmul(dst[:], hi, w_lo, start=False, stop=False)
                nc.tensor.matmul(dst[:], lo, w_hi, start=False, stop=final).then_inc(unit_used, 1)

            pe.wait_ge(consts_ready, CONSTS)
            transposes_to(1)
            pe.wait_ge(norm_ready, 1)
            transpose4(bank[7], lambda t: xn_sb[:, t * P:(t + 1) * P], xpose_ready)

            for u in range(NCTX * TB):
                transposes_to(u + LEAD + 1)
                product(u)

            transposes_to(X_AHEAD)
            for b in range(NCTX):
                pe.wait_ge(x_exp_ready, b + 1)
                transpose4(x_scores[b], lambda t: xp_sb[:, b, t * P:(t + 1) * P], x_pT_ready)
            for b in range(NCTX):
                pe.wait_ge(x_pT_copied, b + 1)
                for t in range(TB):
                    mm = nc.tensor.matmul(x_out[:], xpT_sb[:, b, t * P:(t + 1) * P], raw[:, b % RAW_SLOTS, t, :],
                                          start=(b == 0 and t == 0), stop=(b == NCTX - 1 and t == TB - 1))
                mm.then_inc(x_pv_done, 1)
                if b == 0:
                    transposes_to(KV_AHEAD)
            transposes_to(PV_AHEAD)
            pe.wait_ge(norm_ready, 2)
            transpose4(xpose, lambda t: xn_sb[:, t * P:(t + 1) * P], xpose_ready)

            def transpose_qk(j):
                pe.wait_ge(qk_copied, j + 1)
                pe.wait_ge(xpose_lo_ready, N_LN + j)
                transpose4(xpose, lambda t: qk_sb[:, t * P:(t + 1) * P], xpose_ready)

            def score(g):
                pe.wait_ge(xpose_lo_ready, N_LN + NKV + g + 1)
                if g >= 1:
                    pe.wait_ge(pT_lo_ready, g)
                nc.tensor.matmul(scores[:], ident_b[:], mask[:].rearrange("p g t -> p (g t)"),
                                 start=True, stop=False)
                for h in range(G):
                    s = slice(h * P, (h + 1) * P)
                    nc.tensor.matmul(scores[:, s], qT_hi[:, s], kT_hi[:, g, :], start=False, stop=False)
                    nc.tensor.matmul(scores[:, s], qT_hi[:, s], kT_lo[:, g, :], start=False, stop=False)
                    mm = nc.tensor.matmul(scores[:, s], qT_lo[:, s], kT_hi[:, g, :], start=False,
                                          stop=(h == G - 1))
                mm.then_inc(scored, 1)

            def transpose_probs(g):
                pe.wait_ge(probs_ready, g + 1)
                transpose4(scores, lambda t: pn_sb[:, t, :], pT_ready)

            def values(g):
                pe.wait_ge(pT_lo_ready, g + 1)
                if g == 0:
                    pe.wait_ge(v_lo_ready, NKV)
                else:
                    pe.wait_ge(aT_lo_ready, g)
                nc.tensor.matmul(att_out[:], v_hi[:, g, :], pT_hi[:], start=True, stop=False)
                nc.tensor.matmul(att_out[:], v_hi[:, g, :], pT_lo[:], start=False, stop=False)
                nc.tensor.matmul(att_out[:], v_lo[:, g, :], pT_hi[:], start=False, stop=True).then_inc(att_ready, 1)

            for step in STEPS:
                transposes_to(step + LEAD + 1)
                for kind, i in ended(step, XPOSE):
                    if kind != "v":
                        transpose_qk(QK.index((kind, i)))
                for kind, i in ended(step, SCORE):
                    if kind == "q":
                        score(i)
                for kind, i in ended(step, PROBS):
                    if kind == "q":
                        transpose_probs(i)
                for kind, i in ended(step, VALUES):
                    if kind == "q":
                        values(i)
                product(step)

            pe.wait_ge(norm_ready, 3)
            transpose4(xpose, lambda t: xn_sb[:, t * P:(t + 1) * P], xpose_ready)

            def gate_up(f):
                n = 64 * groups[f]
                if f == 0:
                    pe.wait_ge(xpose_lo_ready, N_LN + len(QK) + 1)
                    for w in range(2):
                        pe.wait_ge(ffn_wt_ready[w], ffn_ops[w])
                if f == NF - 1:
                    pe.wait_ge(h_ready, 1)
                for w, dst, signal in ((0, gate_bank[f], gate_ready), (1, up_bank[f], up_ready)):
                    view = ffn_wt[:, w, :].bitcast(F16).rearrange("p (c i m h) -> p c i m h", c=PC_IN, i=4, h=2)
                    for c in range(TB):
                        mv_w = view[:, c // 2, :, 128 * f:128 * f + n, c % 2]
                        o = dst[:, 0:4 * n].rearrange("p (i m) -> p i m", i=4)
                        nc.tensor.matmul(o, x3T_hi[:, c, :], mv_w, start=(c == 0), stop=False)
                        mm = nc.tensor.matmul(o, x3T_lo[:, c, :], mv_w, start=False, stop=(c == TB - 1))
                    mm.then_inc(signal, 1)

            def transpose_h(f):
                pe.wait_ge(h_ready, f + 1)
                if f >= 2:
                    pe.wait_ge(rest_ready, f - 1)
                for t in range(2 * groups[f]):
                    last = nc.tensor.transpose(hT_bank[f][:, t * P:(t + 1) * P], h_sb[f][:, t * P:(t + 1) * P], ident[:])
                last.then_inc(hT_ready, 1)

            def down(f):
                if f == 0:
                    pe.wait_ge(ffn_wt_ready[2], ffn_ops[2])
                pe.wait_ge(hT_lo_ready, f + 1)
                view = ffn_wt[:, 2, :].bitcast(F16).rearrange("p (c n h) -> p c h n", c=PC_DN, h=2)
                for t in range(2 * groups[f]):
                    w = view[:, 2 * f + t // 2, t % 2, :]
                    for k, part in enumerate((hT_hi, hT_mid, hT_lo)):
                        mm = nc.tensor.matmul(x_out[:], part[f][:, t * P:(t + 1) * P], w,
                                              start=(f == 0 and t == 0 and k == 0),
                                              stop=(f == NF - 1 and t == 2 * groups[f] - 1 and k == 2))
                if f == NF - 1:
                    mm.then_inc(down_done, 1)

            for f in range(NF + 2):
                if f < NF:
                    gate_up(f)
                if 1 <= f <= NF:
                    transpose_h(f - 1)
                if f >= 2:
                    down(f - 2)

        @block.scalar
        def _(act):
            done = [0]

            def highs_to(n):
                for u in range(done[0], min(n, NU)):
                    act.wait_ge(unit_transposed, u + 1)
                    if u >= WT_SLOTS:
                        act.wait_ge(unit_used, u - WT_SLOTS + 1)
                    nc.scalar.activation(wt_hi[:, u % WT_SLOTS, :], tp[u % TP_BANKS][:], ACT.Copy).then_inc(hi_ready, 1)
                done[0] = max(done[0], min(n, NU))

            highs_to(1)
            act.wait_ge(xpose_ready, 1)
            nc.scalar.activation(xT_hi[:].rearrange("p c t -> p (c t)"), bank[7][:], ACT.Copy).then_inc(xpose_hi_ready, 1)
            for u in range(NCTX * TB):
                highs_to(u + LEAD + 1)
            highs_to(X_AHEAD)
            act.wait_ge(x_negmax_ready, 1)
            for b in range(NCTX):
                nc.scalar.activation(xp_sb[:, b, :], x_scores[b][:], ACT.Exp, bias=x_negmax[:, 0:1],
                                     accum_out=x_sum[:, b:b + 1]).then_inc(x_exp_ready, 1)
            highs_to(PV_AHEAD)
            act.wait_ge(xpose_ready, 2)
            nc.scalar.activation(xT_hi[:].rearrange("p c t -> p (c t)"), xpose[:], ACT.Copy).then_inc(xpose_hi_ready, 1)

            for step in STEPS:
                highs_to(step + LEAD + 1)
                for kind, i in ended(step, COPY):
                    act.wait_ge(unit_used, last_unit[kind, i] + 1)
                    if kind == "v":
                        nc.scalar.activation(v_hi[:, TB * i:TB * i + TB, :].rearrange("p h e -> p (h e)"), proj[:],
                                             ACT.Copy).then_inc(v_hi_ready, 1)
                    else:
                        j = QK.index((kind, i))
                        act.wait_ge(xpose_ready, N_LN + j)
                        nc.scalar.activation(qk_sb[:], proj[:], ACT.Copy).then_inc(qk_copied, 1)
                for kind, i in ended(step, XPOSE):
                    if kind == "v":
                        continue
                    act.wait_ge(xpose_ready, N_LN + QK.index((kind, i)) + 1)
                    if kind == "k":
                        hi = kT_hi[:, TB * i:TB * i + TB, :].rearrange("p h t -> p (h t)")
                    else:
                        hi = qT_hi[:]
                        if i >= 1:
                            act.wait_ge(scored, i)
                    nc.scalar.activation(hi, xpose[:], ACT.Copy).then_inc(xpose_hi_ready, 1)
                for kind, i in ended(step, SCORE):
                    if kind != "q":
                        continue
                    act.wait_ge(negmax_ready, i + 1)
                    if i >= 1:
                        act.wait_ge(probs_ready, i)
                    for h in range(G):
                        nc.scalar.activation(p_sb[:, h, :], scores[:, h * P:(h + 1) * P], ACT.Exp,
                                             bias=s_negmax[:, i, h:h + 1], scale=SCALE,
                                             accum_out=s_sum[:, i, h:h + 1]).then_inc(exp_ready, 1)
                for kind, i in ended(step, PROBS):
                    if kind != "q":
                        continue
                    act.wait_ge(pT_ready, i + 1)
                    if i >= 1:
                        act.wait_ge(att_ready, i)
                    nc.scalar.activation(pT_hi[:], scores[:], ACT.Copy).then_inc(pT_hi_ready, 1)
                for kind, i in ended(step, VALUES):
                    if kind != "q":
                        continue
                    act.wait_ge(att_ready, i + 1)
                    if i >= ATT_SLOTS:
                        act.wait_ge(unit_used, last_unit["dense", i - ATT_SLOTS] + 1)
                    nc.scalar.activation(aT_hi[:, i % ATT_SLOTS].rearrange("p h t -> p (h t)"), att_out[:],
                                         ACT.Copy).then_inc(aT_hi_ready, 1)

            act.wait_ge(xpose_ready, N_LN + len(QK) + 1)
            act.wait_ge(unit_transposed, NU)
            nc.scalar.activation(x3T_hi.rearrange("p c t -> p (c t)"), xpose[:], ACT.Copy).then_inc(xpose_hi_ready, 1)

            for f in range(NF + 1):
                if f < NF:
                    n = 256 * groups[f]
                    act.wait_ge(gate_ready, f + 1)
                    nc.scalar.activation(silu_sb[f][:, 0:n], gate_bank[f][:, 0:n], ACT.Silu).then_inc(silu_ready, 1)
                if f >= 1:
                    n = 256 * groups[f - 1]
                    act.wait_ge(hT_ready, f)
                    nc.scalar.activation(hT_hi[f - 1][:, 0:n], hT_bank[f - 1][:, 0:n], ACT.Copy).then_inc(hT_hi_ready, 1)
                    act.wait_ge(rest_ready, f)
                    nc.scalar.activation(hT_mid[f - 1][:, 0:n], hT_rest[f - 1][:, 0:n], ACT.Copy)\
                        .then_inc(hT_mid_ready, 1)

        @block.vector
        def _(dve):
            chain = [0]

            def link(ins):
                chain[0] += 1
                ins.then_inc(dve_done, 1)
                dve.wait_ge(dve_done, chain[0])

            done = [0]

            def lows_to(n):
                for u in range(done[0], min(n, NU)):
                    dve.wait_ge(hi_ready, u + 1)
                    nc.vector.tensor_tensor(wt_lo[:, u % WT_SLOTS, :], tp[u % TP_BANKS][:],
                                            wt_hi[:, u % WT_SLOTS, :].bitcast(F32), ALU.subtract).then_inc(lo_ready, 1)
                done[0] = max(done[0], min(n, NU))

            def paired(v, c):
                return v.rearrange("p (i c a h) -> p c h i a", i=4, c=c, h=2)

            def chunked(v, c):
                return v.rearrange("p (c h i a) -> p c h i a", c=c, h=2, i=4)

            def norm(k, src):
                link(nc.vector.bn_stats(stats[:, k, :], src))
                link(nc.vector.bn_aggr(mv[:, k, :], stats[:, k, :]))
                nc.vector.tensor_scalar(var_eps[:, k:k + 1], mv[:, k, 1:2], EPS, None, ALU.add).then_inc(var_ready, 1)
                dve.wait_ge(rstd_ready, k + 1)
                parts = [(xn_sb[:], src)]
                if k == 2:
                    parts = [(chunked(xn_sb[:], PC_IN)[:, c], paired(src, PC_IN)[:, c]) for c in range(PC_IN)]
                for dst, part in parts:
                    last = nc.vector.tensor_scalar(dst, part, mv[:, k, 0:1], rstd[:, k:k + 1], ALU.subtract, ALU.mult)
                last.then_inc(norm_ready, 1)

            def ffn_transpose(w, n):
                if n == 0:
                    dve.wait_ge(ffn_landed[w], 64)
                    if w >= 1:
                        dve.wait_ge(ffn_wt_ready[w - 1], ffn_ops[w - 1])
                j0, j1 = n * ffn_step_j[w], (n + 1) * ffn_step_j[w]
                pc = ffn_pc[w]
                src = ffn_raw[w].bitcast(U32)[:, j0 * pc * 32:j1 * pc * 32]
                dst = ffn_wt[:, w, :].bitcast(U32).rearrange("p (c j b) -> p j c b", c=pc, b=32)[:, j0:j1]
                nc.vector.transpose(dst, src.rearrange("p (j c a) -> p j c a", c=pc, a=32)).then_inc(ffn_wt_ready[w], 1)

            dve.wait_ge(x_landed, 16)
            norm(0, x_sb[:])
            lows_to(1)
            dve.wait_ge(xpose_hi_ready, 1)
            nc.vector.tensor_tensor(xT_lo[:].rearrange("p c t -> p (c t)"), bank[7][:],
                                    xT_hi[:].rearrange("p c t -> p (c t)").bitcast(F32),
                                    ALU.subtract).then_inc(xpose_lo_ready, 1)
            for u in range(NCTX * TB):
                lows_to(u + LEAD + 1)
                if u % TB == TB - 1:
                    b = u // TB
                    dve.wait_ge(unit_used, u + 1)
                    nc.vector.tensor_reduce(x_max[:, b:b + 1], x_scores[b][:], AX_X, ALU.max).then_inc(dve_done, 1)
                    chain[0] += 1
            dve.wait_ge(dve_done, chain[0])
            link(nc.vector.tensor_reduce(x_negmax[:, 1:2], x_max[:], AX_X, ALU.max))
            nc.vector.tensor_scalar(x_negmax[:, 0:1], x_negmax[:, 1:2], -1.0, None, ALU.mult).then_inc(x_negmax_ready, 1)
            lows_to(X_AHEAD)
            for b in range(NCTX):
                dve.wait_ge(x_pT_ready, b + 1)
                nc.vector.tensor_copy(xpT_sb[:, b, :], x_scores[b][:]).then_inc(x_pT_copied, 1)
            link(nc.vector.tensor_reduce(x_tot[:, 0:1], x_sum[:], AX_X, ALU.add))
            link(nc.vector.reciprocal(x_tot[:, 1:2], x_tot[:, 0:1]))
            lows_to(KV_AHEAD)
            dve.wait_ge(x_pv_done, NCTX)
            link(nc.vector.scalar_tensor_tensor(out=x1_sb[:], in0=x_out[:], scalar=x_tot[:, 1:2], in1=x_sb[:],
                                                op0=ALU.mult, op1=ALU.add))
            norm(1, x1_sb[:])
            lows_to(PV_AHEAD)
            dve.wait_ge(xpose_hi_ready, 2)
            nc.vector.tensor_tensor(xT_lo[:].rearrange("p c t -> p (c t)"), xpose[:],
                                    xT_hi[:].rearrange("p c t -> p (c t)").bitcast(F32),
                                    ALU.subtract).then_inc(xpose_lo_ready, 1)

            for step in STEPS:
                lows_to(step + LEAD + 1)
                for kind, i in ended(step, COPY):
                    if kind == "v":
                        dve.wait_ge(v_hi_ready, i + 1)
                        s = slice(TB * i, TB * i + TB)
                        nc.vector.tensor_tensor(v_lo[:, s, :].rearrange("p h e -> p (h e)"), proj[:],
                                                v_hi[:, s, :].rearrange("p h e -> p (h e)").bitcast(F32),
                                                ALU.subtract).then_inc(v_lo_ready, 1)
                for kind, i in ended(step, XPOSE):
                    if kind == "v":
                        continue
                    dve.wait_ge(xpose_hi_ready, N_LN + QK.index((kind, i)) + 1)
                    if kind == "k":
                        s = slice(TB * i, TB * i + TB)
                        lo, hi = (v[:, s, :].rearrange("p h t -> p (h t)") for v in (kT_lo, kT_hi))
                    else:
                        lo, hi = qT_lo[:], qT_hi[:]
                    nc.vector.tensor_tensor(lo, xpose[:], hi.bitcast(F32), ALU.subtract).then_inc(xpose_lo_ready, 1)
                for kind, i in ended(step, SCORE):
                    if kind != "q":
                        continue
                    dve.wait_ge(scored, i + 1)
                    link(nc.vector.tensor_reduce(s_max[:, i, :], scores[:].rearrange("p (g t) -> p g t", g=G),
                                                 AX_X, ALU.max))
                    nc.vector.tensor_scalar(s_negmax[:, i, :], s_max[:, i, :], -SCALE, None,
                                            ALU.mult).then_inc(negmax_ready, 1)
                if step in ffn_at:
                    ffn_transpose(*ffn_at[step])
                for kind, i in ended(step, SCORE + 2):
                    if kind != "q":
                        continue
                    dve.wait_ge(exp_ready, G * (i + 1))
                    nc.vector.reciprocal(s_inv[:, i, :], s_sum[:, i, :]).then_inc(inv_ready, 1)
                for kind, i in ended(step, PROBS):
                    if kind != "q":
                        continue
                    dve.wait_ge(pT_hi_ready, i + 1)
                    nc.vector.tensor_tensor(pT_lo[:], scores[:], pT_hi[:].bitcast(F32), ALU.subtract)\
                        .then_inc(pT_lo_ready, 1)
                for kind, i in ended(step, VALUES):
                    if kind != "q":
                        continue
                    dve.wait_ge(aT_hi_ready, i + 1)
                    nc.vector.tensor_tensor(aT_lo[:, i % ATT_SLOTS].rearrange("p h t -> p (h t)"), att_out[:],
                                            aT_hi[:, i % ATT_SLOTS].rearrange("p h t -> p (h t)").bitcast(F32),
                                            ALU.subtract).then_inc(aT_lo_ready, 1)

            for n in range(ffn_ops[2]):
                ffn_transpose(2, n)
            dve.wait_ge(unit_used, NU)
            link(nc.vector.tensor_tensor(x2_sb, dense[:], x1_sb[:], ALU.add))
            norm(2, x2_sb)
            dve.wait_ge(xpose_hi_ready, N_LN + len(QK) + 1)
            nc.vector.tensor_tensor(x3T_lo.rearrange("p c t -> p (c t)"), xpose[:],
                                    x3T_hi.rearrange("p c t -> p (c t)"), ALU.subtract).then_inc(xpose_lo_ready, 1)
            for f in range(NF + 1):
                if f < NF:
                    n = 256 * groups[f]
                    dve.wait_ge(silu_ready, f + 1)
                    dve.wait_ge(up_ready, f + 1)
                    c = groups[f]
                    for k in range(c):
                        last = nc.vector.tensor_tensor(chunked(h_sb[f][:, 0:n], c)[:, k],
                                                       paired(up_bank[f][:, 0:n], c)[:, k],
                                                       paired(silu_sb[f][:, 0:n], c)[:, k], ALU.mult)
                    last.then_inc(h_ready, 1)
                if f >= 1:
                    n = 256 * groups[f - 1]
                    dve.wait_ge(hT_hi_ready, f)
                    nc.vector.tensor_tensor(hT_rest[f - 1][:, 0:n], hT_bank[f - 1][:, 0:n], hT_hi[f - 1][:, 0:n],
                                            ALU.subtract).then_inc(rest_ready, 1)
                    dve.wait_ge(hT_mid_ready, f)
                    nc.vector.tensor_tensor(hT_lo[f - 1][:, 0:n], hT_rest[f - 1][:, 0:n], hT_mid[f - 1][:, 0:n],
                                            ALU.subtract).then_inc(hT_lo_ready, 1)
            dve.wait_ge(down_done, 1)
            nc.vector.tensor_tensor(out_sb, x_out[:], x2_sb, ALU.add).then_inc(result_ready, 1)


_INS = ["x", "ctx_4096", "L0_attn_w_qkv", "L0_attn_w_dense", "L0_ffn_W_gate", "L0_ffn_W_up", "L0_ffn_W_down"]


def kernel(**inputs):
    import numpy as np
    import concourse.bacc as bacc
    from concourse.bass_utils import run_bass_kernel_spmd

    nc = bacc.Bacc("TRN2", target_bir_lowering=False, num_devices=1)
    arrays, args = {}, []
    for name in _INS:
        a = np.ascontiguousarray(inputs[name])
        arrays[f"in_{name}"] = a
        args.append(nc.dram_tensor(f"in_{name}", a.shape, mybir.dt.from_np(a.dtype), kind="ExternalInput").ap())
    out = nc.dram_tensor("out", inputs["x"].shape, F32, kind="ExternalOutput").ap()
    perceiver_layer_kernel(nc, *args, out)
    r = run_bass_kernel_spmd(nc, [arrays], core_ids=[0])
    return r.results[0]["out"]
```

```python
from contextlib import ExitStack

import concourse.bass as bass
from concourse import mybir

ALU = mybir.AluOpType
ACT = mybir.ActivationFunctionType
AX_X = mybir.AxisListType.X
F32 = mybir.dt.float32
F32R = mybir.dt.float32r
F16 = mybir.dt.float16
BF16 = mybir.dt.bfloat16
U32 = mybir.dt.uint32

P = 128
TB = 4
RAW_SLOTS = 6
EARLY_SLOTS = 3
AHEAD = 4
WT_SLOTS = 14
TP_BANKS = 3
ATT_SLOTS = 4
LAST_P, LAST_V = 3, 1
LEAD = 3
EPS = 1e-5
MASKED = -1e30


def plan_blocks(n_ctx, n_kv, n_q):
    blocks = [("ctx", i) for i in range(n_ctx)]
    others = [(kind, i) for i in range(n_kv) for kind in "kv"]
    assert len(others) == AHEAD
    for g in range(AHEAD):
        blocks += [others[g], ("q", g)]
    for g in range(AHEAD, n_q):
        blocks += [("dense", g - AHEAD), ("q", g)]
    return blocks + [("dense", g) for g in range(n_q - AHEAD, n_q)]


def perceiver_layer_kernel(nc: bass.Bass, x, ctx_in, w_qkv, w_dense, w_gate, w_up, w_down, out):
    _, S, D = x.shape
    SK = ctx_in.shape[1]
    HD = w_dense.shape[1]
    M = w_gate.shape[0]
    DH = 128
    KVD = (w_qkv.shape[0] - HD) // 2
    KVH = KVD // DH
    G = HD // KVD
    BW = TB * P
    assert S == P and D == BW and G == TB and SK % BW == 0 and M % (4 * 64) == 0
    SCALE = float(DH) ** -0.5
    NCTX, NKV, NQ = SK // BW, KVD // BW, HD // BW

    BLOCKS = plan_blocks(NCTX, NKV, NQ)
    NB = len(BLOCKS)
    EARLY_BLOCKS = RAW_SLOTS + EARLY_SLOTS
    NU = NB * TB
    last_unit = {k: b * TB + TB - 1 for b, k in enumerate(BLOCKS)}

    PC_IN = D // 4 // 64
    PC_DN = M // 4 // 64
    JG, JD = M // 32, D // 32
    NF = -(-PC_DN // 2)

    with ExitStack() as ctx:
        def sb(name, shape, dt=F32):
            return ctx.enter_context(nc.sbuf_tensor(name, shape, dt))

        def sem(name):
            return ctx.enter_context(nc.semaphore(name))

        raw = sb("raw", [P, RAW_SLOTS, TB, BW])
        wt_hi = sb("wt_hi", [P, WT_SLOTS, BW], F32R)
        wt_lo = sb("wt_lo", [P, WT_SLOTS, BW], F32R)
        ffn_wt = sb("ffn_wt", [P, 3, M * 2])
        x_sb = sb("x_sb", [P, D])
        x1_sb = sb("x1_sb", [P, D])
        xn_sb = sb("xn_sb", [P, D])
        xT_hi = sb("xT_hi", [P, TB, P], F32R)
        xT_lo = sb("xT_lo", [P, TB, P], F32R)
        kT = sb("kT", [P, KVH, P])
        v_hi = sb("v_hi", [P, KVH, P], F32R)
        v_lo = sb("v_lo", [P, KVH, P], F32R)
        qk_sb = sb("qk_sb", [P, BW])
        qT = sb("qT", [P, G * P])
        p_sb = sb("p_sb", [P, G, P])
        pT_hi = sb("pT_hi", [P, G * P], F32R)
        pT_lo = sb("pT_lo", [P, G * P], F32R)
        aT_hi = sb("aT_hi", [P, ATT_SLOTS, G, P], F32R)
        aT_lo = sb("aT_lo", [P, ATT_SLOTS, G, P], F32R)
        ident = sb("ident", [P, P])
        ident_b = sb("ident_b", [P, P], BF16)
        mask = sb("mask", [P, G, P], BF16)
        stats = sb("stats", [P, 3, 6])
        mv = sb("mv", [P, 3, 2])
        rstd = sb("rstd", [P, 3])
        var_eps = sb("var_eps", [P, 3])
        minus_half = sb("minus_half", [P, 1])
        x_max = sb("x_max", [P, NCTX])
        x_negmax = sb("x_negmax", [P, 2])
        x_sum = sb("x_sum", [P, NCTX])
        x_tot = sb("x_tot", [P, 2])
        s_max = sb("s_max", [P, NQ, G])
        s_negmax = sb("s_negmax", [P, NQ, G])
        s_sum = sb("s_sum", [P, NQ, G])
        s_inv = sb("s_inv", [P, NQ, G])

        flat = ffn_wt[:].rearrange("p a b -> p (a b)")
        xp_sb = flat[:, 0:SK].rearrange("p (b n) -> p b n", b=NCTX)
        xpT_sb = flat[:, SK:2 * SK].rearrange("p (b n) -> p b n", b=NCTX)
        early = flat[:, 2 * SK:2 * SK + EARLY_SLOTS * TB * BW].rearrange("p (s t n) -> p s t n", s=EARLY_SLOTS, t=TB)

        def raw_slot(b):
            if b < EARLY_BLOCKS:
                return b, (raw[:, b] if b < RAW_SLOTS else early[:, b - RAW_SLOTS]), None
            s = (b - EARLY_BLOCKS) % RAW_SLOTS
            return s, raw[:, s], (b - EARLY_BLOCKS if b < EARLY_BLOCKS + RAW_SLOTS else b - RAW_SLOTS)

        def raw_count(b):
            before = raw_slot(b)[2]
            return (0 if b == 0 else 16) if before is None else 16 + raw_count(before)

        GROW = M * 2
        area = raw[:].rearrange("p s t n -> p (s t n)")
        down_at = ((NB - 6 - EARLY_BLOCKS) % RAW_SLOTS) * TB * BW
        down_raw = area[:, down_at:down_at + GROW]
        x2_sb, out_sb = area[:, 0:D], area[:, D:2 * D]
        x3T_hi, x3T_lo = (area[:, n * D:n * D + D // 2].bitcast(F16).rearrange("p (c t) -> p c t", c=TB)
                          for n in (2, 3))
        silu_sb = [area[:, (4 + f) * D:(5 + f) * D] for f in range(NF)]
        h_sb = [area[:, (8 + f) * D:(9 + f) * D] for f in range(NF)]
        assert 12 * D <= down_at and 2 * PC_DN <= WT_SLOTS and 2 * NF <= WT_SLOTS
        down_w = wt_hi
        hT_hi, hT_lo = wt_lo[:, 0:NF], wt_lo[:, NF:2 * NF]

        bank = [ctx.enter_context(nc.psum_tensor(f"bank{i}", [P, BW], F32)) for i in range(8)]
        tp = bank[0:TP_BANKS]
        x_scores = bank[3:3 + NCTX]
        x_out = bank[7]
        scores, xpose, att_out, dense = bank[4:8]

        def proj_bank(n):
            return dense if n % 2 == 0 and n < 2 * NKV + AHEAD else bank[3]

        raw_landed = [sem(f"raw_landed{i}") for i in range(EARLY_BLOCKS)]
        ctx0_landed = [sem(f"ctx0_landed{c}") for c in range(TB)]
        x_landed = sem("x_landed")
        ffn_landed = [sem(f"ffn_landed{i}") for i in range(3)]
        out_stored = sem("out_stored")
        consts_ready = sem("consts_ready")
        unit_transposed = sem("unit_transposed")
        hi_ready = sem("hi_ready")
        lo_ready = sem("lo_ready")
        unit_used = sem("unit_used")
        var_ready = sem("var_ready")
        rstd_ready = sem("rstd_ready")
        norm_ready = sem("norm_ready")
        xpose_ready = sem("xpose_ready")
        normT_hi_ready = sem("normT_hi_ready")
        normT_lo_ready = sem("normT_lo_ready")
        qkT_ready = sem("qkT_ready")
        x_negmax_ready = sem("x_negmax_ready")
        x_exp_ready = sem("x_exp_ready")
        x_pT_ready = sem("x_pT_ready")
        x_pT_copied = sem("x_pT_copied")
        x_pv_done = sem("x_pv_done")
        qk_copied = sem("qk_copied")
        v_hi_ready = sem("v_hi_ready")
        v_lo_ready = sem("v_lo_ready")
        scored = sem("scored")
        negmax_ready = sem("negmax_ready")
        exp_ready = sem("exp_ready")
        inv_ready = sem("inv_ready")
        probs_ready = sem("probs_ready")
        pT_ready = sem("pT_ready")
        pT_hi_ready = sem("pT_hi_ready")
        pT_lo_ready = sem("pT_lo_ready")
        att_ready = sem("att_ready")
        aT_hi_ready = sem("aT_hi_ready")
        aT_lo_ready = sem("aT_lo_ready")
        dve_done = sem("dve_done")
        ffn_wt_ready = [sem(f"ffn_wt_ready{i}") for i in range(3)]
        gate_ready = sem("gate_ready")
        up_ready = sem("up_ready")
        silu_ready = sem("silu_ready")
        h_ready = sem("h_ready")
        hT_ready = sem("hT_ready")
        hT_hi_ready = sem("hT_hi_ready")
        down_w_ready = sem("down_w_ready")
        hT_lo_ready = sem("hT_lo_ready")
        down_done = sem("down_done")
        result_ready = sem("result_ready")

        def block_src(kind, i):
            if kind == "dense":
                return w_dense[:, i * BW:(i + 1) * BW].rearrange("(t p) n -> p t n", p=P)
            rows = {"ctx": ctx_in[0], "q": w_qkv[0:HD], "k": w_qkv[HD:HD + KVD], "v": w_qkv[HD + KVD:]}[kind]
            return rows[i * BW:(i + 1) * BW].rearrange("(t p) n -> p t n", p=P)

        ffn_raw = [ffn_wt[:, 1, :], ffn_wt[:, 2, :], down_raw]
        ffn_dram = [w_gate, w_up, w_down]
        ffn_pc = [PC_IN, PC_IN, PC_DN]
        ffn_j = [JG, JG, JD]
        ffn_step_j = [512 // (32 * pc) for pc in ffn_pc]
        ffn_ops = [j // s for j, s in zip(ffn_j, ffn_step_j)]

        def ffn_view(w, part):
            return ffn_wt[:, w, :].bitcast(F16).rearrange("p (c n h) -> p c n h", c=ffn_pc[w], h=2)[part]

        PROJ = [k for k in BLOCKS if k[0] in "kvq"]
        QK = [k for k in PROJ if k[0] != "v"]
        COPY, XPOSE, SCORE, INVERSE, PROBS, VALUES = range(6)
        when = {}
        for k in PROJ:
            when[k, COPY], when[k, XPOSE] = last_unit[k] + 1, last_unit[k] + 2
            if k[0] == "q":
                before = ("q", k[1] - 1)
                if k[1] > 0:
                    when[k, XPOSE] = max(when[k, XPOSE], when[before, SCORE] + 1)
                    when[k, COPY] = max(when[k, COPY], when[before, XPOSE] + 1)
                when[k, SCORE] = when[k, XPOSE] + 3
                if k[1] > 0:
                    when[k, SCORE] = max(when[k, SCORE], when[before, PROBS])
                when[k, INVERSE] = when[k, SCORE] + 3
                due_by = last_unit["dense", k[1]] - TB + 1
                when[k, PROBS] = min(when[k, SCORE] + 7, due_by - LAST_P)
                when[k, VALUES] = min(when[k, PROBS] + 3, due_by - LAST_V)
        X_AHEAD = NCTX * TB + LEAD + 2
        KV_AHEAD = (NCTX + NKV) * TB
        PV_AHEAD = NCTX * TB + WT_SLOTS
        STEPS = range(NCTX * TB, NU)
        N_LN = 2

        def due(step, stage):
            return [k for k in PROJ if when.get((k, stage)) == step]

        ffn_at = {TB * (NB - 9) + n: (0, n) for n in range(ffn_ops[0])}
        ffn_at |= {TB * (NB - 6) + n: (1, n) for n in range(ffn_ops[1])}
        ffn_at |= {TB * NB - ffn_ops[2] + n: (2, n) for n in range(ffn_ops[2])}
        FFN_AT = EARLY_BLOCKS + RAW_SLOTS

        groups = [min(2, PC_DN - 2 * f) for f in range(NF)]
        gate_bank = [bank[i] for i in (0, 2, 4, 0)]
        up_bank = [bank[i] for i in (1, 3, 6, 1)]
        hT_bank = [bank[i] for i in (5, 2, 5, 2)]

        block = ctx.enter_context(nc.Block())

        @block.sync
        def _(sp):
            sp.dma_start(x_sb[:], x[0]).then_inc(x_landed, 16)

            def load_ffn(w, i):
                pc = ffn_pc[w]
                dst = ffn_raw[w].bitcast(F16).rearrange("p (j d) -> p j d", j=ffn_j[w])
                src = ffn_dram[w][:, i * pc * 64:(i + 1) * pc * 64].rearrange("(j b) d -> b j d", b=32)
                sp.dma_start(dst[32 * i:32 * i + 32], src).then_inc(ffn_landed[w], 16)

            for b, (kind, i) in enumerate(BLOCKS):
                slot, dst, old = raw_slot(b)
                if old is not None and BLOCKS[old][0] == "ctx":
                    sp.wait_ge(x_pv_done, old + 1)
                elif old is not None:
                    sp.wait_ge(unit_transposed, TB * (old + 1))
                if 0 <= b - FFN_AT < 8:
                    load_ffn(*divmod(b - FFN_AT, 4))
                if b == NB - 1:
                    sp.wait_ge(unit_transposed, TB * (NB - 4))
                    for q in range(4):
                        load_ffn(2, q)
                src = block_src(kind, i)
                if b == 0:
                    for c in range(TB):
                        s = slice(c * P, (c + 1) * P)
                        sp.dma_start(dst[:, :, s], src[:, :, s]).then_inc(ctx0_landed[c], 16)
                else:
                    sp.dma_start(dst, src).then_inc(raw_landed[slot], 16)
            sp.wait_ge(result_ready, 1)
            sp.dma_start(out[0], out_sb).then_inc(out_stored, 16)
            sp.wait_ge(out_stored, 16)

        CONSTS = 7

        @block.gpsimd
        def _(pool):
            def inverse_root(k):
                pool.wait_ge(var_ready, k + 1)
                nc.gpsimd.tensor_tensor(rstd[:, k:k + 1], var_eps[:, k:k + 1], minus_half[:],
                                        ALU.pow).then_inc(rstd_ready, 1)

            nc.gpsimd.memset(minus_half[:], -0.5).then_inc(consts_ready, 1)
            nc.gpsimd.memset(ident[:], 0.0).then_inc(consts_ready, 1)
            nc.gpsimd.memset(ident_b[:], 0.0).then_inc(consts_ready, 1)
            nc.gpsimd.memset(mask[:], 0.0).then_inc(consts_ready, 1)
            pool.wait_ge(consts_ready, 4)
            for m in (ident, ident_b):
                nc.gpsimd.affine_select(out=m[:], in_=m[:], compare_op=ALU.not_equal, fill=1.0, base=0,
                                        pattern=[[-1, P]], channel_multiplier=1).then_inc(consts_ready, 1)
            nc.gpsimd.affine_select(out=mask[:], in_=mask[:], compare_op=ALU.is_ge, fill=MASKED, base=0,
                                    pattern=[[0, G], [-1, P]], channel_multiplier=1).then_inc(consts_ready, 1)
            inverse_root(0)
            inverse_root(1)
            for g in range(NQ):
                pool.wait_ge(inv_ready, g + 1)
                nc.gpsimd.tensor_tensor(p_sb[:], p_sb[:], s_inv[:, g, :].unsqueeze(2).to_broadcast([P, G, P]),
                                        ALU.mult).then_inc(probs_ready, 1)
            inverse_root(2)

        @block.tensor
        def _(pe):
            done = [0]

            def transposes_to(n):
                for u in range(done[0], min(n, NU)):
                    b, c = divmod(u, TB)
                    slot, src, _ = raw_slot(b)
                    if b == 0:
                        pe.wait_ge(ctx0_landed[c], 16)
                    elif c == 0:
                        pe.wait_ge(raw_landed[slot], raw_count(b))
                    if u >= TP_BANKS:
                        pe.wait_ge(lo_ready, u - TP_BANKS + 1)
                    for t in range(TB):
                        last = nc.tensor.transpose(tp[u % TP_BANKS][:, t * P:(t + 1) * P],
                                                   src[:, t, c * P:(c + 1) * P], ident[:])
                    last.then_inc(unit_transposed, 1)
                done[0] = max(done[0], min(n, NU))

            def transpose4(dst, tile_of, signal):
                for t in range(TB):
                    last = nc.tensor.transpose(dst[:, t * P:(t + 1) * P], tile_of(t), ident[:])
                last.then_inc(signal, 1)

            def left(n):
                kind, i = PROJ[n]
                if kind == "v":
                    pe.wait_ge(v_lo_ready, i + 1)
                else:
                    pe.wait_ge(qk_copied, QK.index(PROJ[n]) + 1)

            def product(u):
                b, c = divmod(u, TB)
                kind, i = BLOCKS[b]
                first, final = c == 0, c == TB - 1
                if kind == "dense":
                    hi, lo, dst = aT_hi[:, i % ATT_SLOTS, c, :], aT_lo[:, i % ATT_SLOTS, c, :], dense
                    first, final = first and i == 0, final and i == NQ - 1
                    if c == 0:
                        pe.wait_ge(aT_lo_ready, i + 1)
                    if first:
                        left(2 * NKV + AHEAD - 2)
                elif kind == "ctx":
                    hi, lo, dst = xT_hi[:, c, :], xT_lo[:, c, :], x_scores[i]
                    if u == 0:
                        pe.wait_ge(normT_lo_ready, 1)
                else:
                    n = PROJ.index((kind, i))
                    hi, lo, dst = xT_hi[:, c, :], xT_lo[:, c, :], proj_bank(n)
                    if c == 0 and n == 0:
                        pe.wait_ge(normT_lo_ready, 2)
                    elif c == 0 and n >= 2:
                        left(n - 1 if proj_bank(n) is proj_bank(n - 1) else n - 2)
                pe.wait_ge(lo_ready, u + 1)
                w_hi, w_lo = wt_hi[:, u % WT_SLOTS, :], wt_lo[:, u % WT_SLOTS, :]
                nc.tensor.matmul(dst[:], hi, w_hi, start=first, stop=False)
                nc.tensor.matmul(dst[:], hi, w_lo, start=False, stop=False)
                nc.tensor.matmul(dst[:], lo, w_hi, start=False, stop=final).then_inc(unit_used, 1)

            pe.wait_ge(consts_ready, CONSTS)
            transposes_to(1)
            pe.wait_ge(norm_ready, 1)
            transpose4(bank[7], lambda t: xn_sb[:, t * P:(t + 1) * P], xpose_ready)

            for u in range(NCTX * TB):
                transposes_to(u + LEAD + 1)
                product(u)

            transposes_to(X_AHEAD)
            for b in range(NCTX):
                pe.wait_ge(x_exp_ready, b + 1)
                transpose4(x_scores[b], lambda t: xp_sb[:, b, t * P:(t + 1) * P], x_pT_ready)
            for b in range(NCTX):
                pe.wait_ge(x_pT_copied, b + 1)
                for t in range(TB):
                    mm = nc.tensor.matmul(x_out[:], xpT_sb[:, b, t * P:(t + 1) * P], raw[:, b, t, :],
                                          start=(b == 0 and t == 0), stop=(b == NCTX - 1 and t == TB - 1))
                mm.then_inc(x_pv_done, 1)
                if b == 0:
                    transposes_to(KV_AHEAD)
                if b == NCTX - 2:
                    transposes_to(KV_AHEAD + TP_BANKS)
            transposes_to(PV_AHEAD)
            pe.wait_ge(norm_ready, 2)
            transpose4(xpose, lambda t: xn_sb[:, t * P:(t + 1) * P], xpose_ready)

            transposed = {"qk": 0, "probs": 0}

            def xpose_left():
                if transposed["qk"] > 0:
                    pe.wait_ge(qkT_ready, transposed["qk"])
                if transposed["probs"] > 0:
                    pe.wait_ge(pT_lo_ready, transposed["probs"])

            def transpose_qk(j):
                pe.wait_ge(qk_copied, j + 1)
                xpose_left()
                transposed["qk"] += 1
                transpose4(xpose, lambda t: qk_sb[:, t * P:(t + 1) * P], xpose_ready)

            def score(g):
                pe.wait_ge(qkT_ready, QK.index(("q", g)) + 1)
                if g >= 1:
                    pe.wait_ge(exp_ready, G * g)
                nc.tensor.matmul(scores[:], ident_b[:], mask[:].rearrange("p g t -> p (g t)"),
                                 start=True, stop=False)
                for h in range(G):
                    s = slice(h * P, (h + 1) * P)
                    mm = nc.tensor.matmul(scores[:, s], qT[:, s], kT[:, g, :], start=False, stop=(h == G - 1))
                mm.then_inc(scored, 1)

            def transpose_probs(g):
                pe.wait_ge(probs_ready, g + 1)
                xpose_left()
                transposed["probs"] += 1
                transpose4(xpose, lambda t: p_sb[:, t, :], pT_ready)

            def values(g):
                pe.wait_ge(pT_lo_ready, g + 1)
                if g % TB == 0:
                    pe.wait_ge(v_lo_ready, g // TB + 1)
                if g >= 1:
                    pe.wait_ge(aT_lo_ready, g)
                nc.tensor.matmul(att_out[:], v_hi[:, g, :], pT_hi[:], start=True, stop=False)
                nc.tensor.matmul(att_out[:], v_hi[:, g, :], pT_lo[:], start=False, stop=False)
                nc.tensor.matmul(att_out[:], v_lo[:, g, :], pT_hi[:], start=False, stop=True).then_inc(att_ready, 1)

            for step in STEPS:
                transposes_to(step + LEAD + 1)
                for kind, i in due(step, XPOSE):
                    if kind != "v":
                        transpose_qk(QK.index((kind, i)))
                for kind, i in due(step, SCORE):
                    if kind == "q":
                        score(i)
                for kind, i in due(step, PROBS):
                    if kind == "q":
                        transpose_probs(i)
                for kind, i in due(step, VALUES):
                    if kind == "q":
                        values(i)
                product(step)

            pe.wait_ge(norm_ready, 3)
            xpose_left()
            transpose4(xpose, lambda t: xn_sb[:, t * P:(t + 1) * P], xpose_ready)

            def gate_up(f):
                n = 64 * groups[f]
                if f == 0:
                    pe.wait_ge(normT_lo_ready, 3)
                    for w in range(2):
                        pe.wait_ge(ffn_wt_ready[w], ffn_ops[w])
                if f == NF - 1:
                    pe.wait_ge(h_ready, 1)
                for w, dst, signal in ((0, gate_bank[f], gate_ready), (1, up_bank[f], up_ready)):
                    view = ffn_wt[:, w, :].bitcast(F16).rearrange("p (c i m h) -> p c i m h", c=PC_IN, i=4, h=2)
                    for c in range(TB):
                        mv_w = view[:, c // 2, :, 128 * f:128 * f + n, c % 2]
                        o = dst[:, 0:4 * n].rearrange("p (i m) -> p i m", i=4)
                        nc.tensor.matmul(o, x3T_hi[:, c, :], mv_w, start=(c == 0), stop=False)
                        mm = nc.tensor.matmul(o, x3T_lo[:, c, :], mv_w, start=False, stop=(c == TB - 1))
                    mm.then_inc(signal, 1)

            def transpose_h(f):
                pe.wait_ge(h_ready, f + 1)
                if f >= 2:
                    pe.wait_ge(hT_lo_ready, f - 1)
                for t in range(2 * groups[f]):
                    last = nc.tensor.transpose(hT_bank[f][:, t * P:(t + 1) * P], h_sb[f][:, t * P:(t + 1) * P], ident[:])
                last.then_inc(hT_ready, 1)

            def down(f):
                pe.wait_ge(hT_lo_ready, f + 1)
                for t in range(2 * groups[f]):
                    k = 4 * f + t
                    pe.wait_ge(down_w_ready, k + 1)
                    nc.tensor.matmul(x_out[:], hT_hi[:, f, t * P:(t + 1) * P], down_w[:, k, :], start=(k == 0), stop=False)
                    mm = nc.tensor.matmul(x_out[:], hT_lo[:, f, t * P:(t + 1) * P], down_w[:, k, :], start=False,
                                          stop=(k == 2 * PC_DN - 1))
                if f == NF - 1:
                    mm.then_inc(down_done, 1)

            for f in range(NF + 2):
                if f < NF:
                    gate_up(f)
                if 1 <= f <= NF:
                    transpose_h(f - 1)
                if f >= 2:
                    down(f - 2)

        @block.scalar
        def _(act):
            done = [0]

            def highs_to(n):
                for u in range(done[0], min(n, NU)):
                    act.wait_ge(unit_transposed, u + 1)
                    if u >= WT_SLOTS:
                        act.wait_ge(unit_used, u - WT_SLOTS + 1)
                    nc.scalar.activation(wt_hi[:, u % WT_SLOTS, :], tp[u % TP_BANKS][:], ACT.Copy).then_inc(hi_ready, 1)
                done[0] = max(done[0], min(n, NU))

            highs_to(1)
            act.wait_ge(xpose_ready, 1)
            nc.scalar.activation(xT_hi[:].rearrange("p c t -> p (c t)"), bank[7][:], ACT.Copy).then_inc(normT_hi_ready, 1)
            for u in range(NCTX * TB):
                highs_to(u + LEAD + 1)
            highs_to(X_AHEAD)
            act.wait_ge(x_negmax_ready, 1)
            for b in range(NCTX):
                nc.scalar.activation(xp_sb[:, b, :], x_scores[b][:], ACT.Exp, bias=x_negmax[:, 0:1],
                                     accum_out=x_sum[:, b:b + 1]).then_inc(x_exp_ready, 1)
            highs_to(PV_AHEAD)
            act.wait_ge(xpose_ready, 2)
            nc.scalar.activation(xT_hi[:].rearrange("p c t -> p (c t)"), xpose[:], ACT.Copy).then_inc(normT_hi_ready, 1)

            for step in STEPS:
                highs_to(step + LEAD + 1)
                for kind, i in due(step, COPY):
                    act.wait_ge(unit_used, last_unit[kind, i] + 1)
                    src = proj_bank(PROJ.index((kind, i)))
                    if kind == "v":
                        nc.scalar.activation(v_hi[:, TB * i:TB * i + TB, :].rearrange("p h e -> p (h e)"), src[:],
                                             ACT.Copy).then_inc(v_hi_ready, 1)
                    else:
                        j = QK.index((kind, i))
                        act.wait_ge(xpose_ready, N_LN + j)
                        nc.scalar.activation(qk_sb[:], src[:], ACT.Copy).then_inc(qk_copied, 1)
                for kind, i in due(step, XPOSE):
                    if kind == "v":
                        continue
                    act.wait_ge(xpose_ready, N_LN + QK.index((kind, i)) + 1)
                    if kind == "k":
                        dst = kT[:, TB * i:TB * i + TB, :].rearrange("p h t -> p (h t)")
                    else:
                        dst = qT[:]
                        if i >= 1:
                            act.wait_ge(scored, i)
                    nc.scalar.activation(dst, xpose[:], ACT.Copy).then_inc(qkT_ready, 1)
                for kind, i in due(step, SCORE):
                    if kind != "q":
                        continue
                    act.wait_ge(negmax_ready, i + 1)
                    if i >= 1:
                        act.wait_ge(pT_ready, i)
                    for h in range(G):
                        nc.scalar.activation(p_sb[:, h, :], scores[:, h * P:(h + 1) * P], ACT.Exp,
                                             bias=s_negmax[:, i, h:h + 1], scale=SCALE,
                                             accum_out=s_sum[:, i, h:h + 1]).then_inc(exp_ready, 1)
                for kind, i in due(step, PROBS):
                    if kind != "q":
                        continue
                    act.wait_ge(pT_ready, i + 1)
                    if i >= 1:
                        act.wait_ge(att_ready, i)
                    nc.scalar.activation(pT_hi[:], xpose[:], ACT.Copy).then_inc(pT_hi_ready, 1)
                for kind, i in due(step, VALUES):
                    if kind != "q":
                        continue
                    act.wait_ge(att_ready, i + 1)
                    if i >= ATT_SLOTS:
                        act.wait_ge(unit_used, last_unit["dense", i - ATT_SLOTS] + 1)
                    nc.scalar.activation(aT_hi[:, i % ATT_SLOTS].rearrange("p h t -> p (h t)"), att_out[:],
                                         ACT.Copy).then_inc(aT_hi_ready, 1)

            act.wait_ge(xpose_ready, N_LN + len(QK) + 1)
            act.wait_ge(unit_transposed, NU)
            nc.scalar.activation(x3T_hi.rearrange("p c t -> p (c t)"), xpose[:], ACT.Copy).then_inc(normT_hi_ready, 1)

            act.wait_ge(ffn_wt_ready[2], ffn_ops[2])
            view = ffn_wt[:, 2, :].bitcast(F16).rearrange("p (c n h) -> p c h n", c=PC_DN, h=2)

            def down_weights(k0, k1):
                for k in range(k0, min(k1, 2 * PC_DN)):
                    nc.scalar.activation(down_w[:, k, :], view[:, k // 2, k % 2, :], ACT.Copy).then_inc(down_w_ready, 1)

            down_weights(0, 7)
            for f in range(NF + 1):
                if f < NF:
                    n = 256 * groups[f]
                    act.wait_ge(gate_ready, f + 1)
                    nc.scalar.activation(silu_sb[f][:, 0:n], gate_bank[f][:, 0:n], ACT.Silu).then_inc(silu_ready, 1)
                if f >= 1:
                    n = 256 * groups[f - 1]
                    act.wait_ge(hT_ready, f)
                    nc.scalar.activation(hT_hi[:, f - 1, 0:n], hT_bank[f - 1][:, 0:n], ACT.Copy).then_inc(hT_hi_ready, 1)
                down_weights(7 + 3 * f, 10 + 3 * f)

        @block.vector
        def _(dve):
            chain = [0]

            def link(ins):
                chain[0] += 1
                ins.then_inc(dve_done, 1)
                dve.wait_ge(dve_done, chain[0])

            done = [0]

            def lows_to(n):
                for u in range(done[0], min(n, NU)):
                    dve.wait_ge(hi_ready, u + 1)
                    nc.vector.tensor_tensor(wt_lo[:, u % WT_SLOTS, :], tp[u % TP_BANKS][:],
                                            wt_hi[:, u % WT_SLOTS, :].bitcast(F32), ALU.subtract).then_inc(lo_ready, 1)
                done[0] = max(done[0], min(n, NU))

            def paired(v, c):
                return v.rearrange("p (i c a h) -> p c h i a", i=4, c=c, h=2)

            def chunked(v, c):
                return v.rearrange("p (c h i a) -> p c h i a", c=c, h=2, i=4)

            def norm(k, src):
                link(nc.vector.bn_stats(stats[:, k, :], src))
                link(nc.vector.bn_aggr(mv[:, k, :], stats[:, k, :]))
                nc.vector.tensor_scalar(var_eps[:, k:k + 1], mv[:, k, 1:2], EPS, None, ALU.add).then_inc(var_ready, 1)
                dve.wait_ge(rstd_ready, k + 1)
                parts = [(xn_sb[:], src)]
                if k == 2:
                    parts = [(chunked(xn_sb[:], PC_IN)[:, c], paired(src, PC_IN)[:, c]) for c in range(PC_IN)]
                for dst, part in parts:
                    last = nc.vector.tensor_scalar(dst, part, mv[:, k, 0:1], rstd[:, k:k + 1], ALU.subtract, ALU.mult)
                last.then_inc(norm_ready, 1)

            def ffn_transpose(w, n):
                if n == 0:
                    dve.wait_ge(ffn_landed[w], 64)
                    if w >= 1:
                        dve.wait_ge(ffn_wt_ready[w - 1], ffn_ops[w - 1])
                j0, j1 = n * ffn_step_j[w], (n + 1) * ffn_step_j[w]
                pc = ffn_pc[w]
                src = ffn_raw[w].bitcast(U32)[:, j0 * pc * 32:j1 * pc * 32]
                dst = ffn_wt[:, w, :].bitcast(U32).rearrange("p (c j b) -> p j c b", c=pc, b=32)[:, j0:j1]
                nc.vector.transpose(dst, src.rearrange("p (j c a) -> p j c a", c=pc, a=32)).then_inc(ffn_wt_ready[w], 1)

            dve.wait_ge(x_landed, 16)
            norm(0, x_sb[:])
            lows_to(1)
            dve.wait_ge(normT_hi_ready, 1)
            nc.vector.tensor_tensor(xT_lo[:].rearrange("p c t -> p (c t)"), bank[7][:],
                                    xT_hi[:].rearrange("p c t -> p (c t)").bitcast(F32),
                                    ALU.subtract).then_inc(normT_lo_ready, 1)
            for u in range(NCTX * TB):
                lows_to(u + LEAD + 1)
                if u % TB == TB - 1:
                    b = u // TB
                    dve.wait_ge(unit_used, u + 1)
                    nc.vector.tensor_reduce(x_max[:, b:b + 1], x_scores[b][:], AX_X, ALU.max).then_inc(dve_done, 1)
                    chain[0] += 1
            dve.wait_ge(dve_done, chain[0])
            link(nc.vector.tensor_reduce(x_negmax[:, 1:2], x_max[:], AX_X, ALU.max))
            nc.vector.tensor_scalar(x_negmax[:, 0:1], x_negmax[:, 1:2], -1.0, None, ALU.mult).then_inc(x_negmax_ready, 1)
            lows_to(X_AHEAD)
            for b in range(NCTX):
                dve.wait_ge(x_pT_ready, b + 1)
                nc.vector.tensor_copy(xpT_sb[:, b, :], x_scores[b][:]).then_inc(x_pT_copied, 1)
            link(nc.vector.tensor_reduce(x_tot[:, 0:1], x_sum[:], AX_X, ALU.add))
            link(nc.vector.reciprocal(x_tot[:, 1:2], x_tot[:, 0:1]))
            lows_to(KV_AHEAD + TP_BANKS)
            dve.wait_ge(x_pv_done, NCTX)
            link(nc.vector.scalar_tensor_tensor(out=x1_sb[:], in0=x_out[:], scalar=x_tot[:, 1:2], in1=x_sb[:],
                                                op0=ALU.mult, op1=ALU.add))
            norm(1, x1_sb[:])
            dve.wait_ge(normT_hi_ready, 2)
            nc.vector.tensor_tensor(xT_lo[:].rearrange("p c t -> p (c t)"), xpose[:],
                                    xT_hi[:].rearrange("p c t -> p (c t)").bitcast(F32),
                                    ALU.subtract).then_inc(normT_lo_ready, 1)

            for step in STEPS:
                lows_to(step + LEAD + 1)
                for kind, i in due(step, COPY):
                    if kind == "v":
                        dve.wait_ge(v_hi_ready, i + 1)
                        s = slice(TB * i, TB * i + TB)
                        nc.vector.tensor_tensor(v_lo[:, s, :].rearrange("p h e -> p (h e)"),
                                                proj_bank(PROJ.index((kind, i)))[:],
                                                v_hi[:, s, :].rearrange("p h e -> p (h e)").bitcast(F32),
                                                ALU.subtract).then_inc(v_lo_ready, 1)
                for kind, i in due(step, SCORE):
                    if kind != "q":
                        continue
                    dve.wait_ge(scored, i + 1)
                    link(nc.vector.tensor_reduce(s_max[:, i, :], scores[:].rearrange("p (g t) -> p g t", g=G),
                                                 AX_X, ALU.max))
                    nc.vector.tensor_scalar(s_negmax[:, i, :], s_max[:, i, :], -SCALE, None,
                                            ALU.mult).then_inc(negmax_ready, 1)
                if step in ffn_at:
                    ffn_transpose(*ffn_at[step])
                for kind, i in due(step, INVERSE):
                    if kind != "q":
                        continue
                    dve.wait_ge(exp_ready, G * (i + 1))
                    nc.vector.reciprocal(s_inv[:, i, :], s_sum[:, i, :]).then_inc(inv_ready, 1)
                for kind, i in due(step, PROBS):
                    if kind != "q":
                        continue
                    dve.wait_ge(pT_hi_ready, i + 1)
                    nc.vector.tensor_tensor(pT_lo[:], xpose[:], pT_hi[:].bitcast(F32), ALU.subtract)\
                        .then_inc(pT_lo_ready, 1)
                for kind, i in due(step, VALUES):
                    if kind != "q":
                        continue
                    dve.wait_ge(aT_hi_ready, i + 1)
                    nc.vector.tensor_tensor(aT_lo[:, i % ATT_SLOTS].rearrange("p h t -> p (h t)"), att_out[:],
                                            aT_hi[:, i % ATT_SLOTS].rearrange("p h t -> p (h t)").bitcast(F32),
                                            ALU.subtract).then_inc(aT_lo_ready, 1)

            dve.wait_ge(unit_used, NU)
            link(nc.vector.tensor_tensor(x2_sb, dense[:], x1_sb[:], ALU.add))
            norm(2, x2_sb)
            dve.wait_ge(normT_hi_ready, 3)
            nc.vector.tensor_tensor(x3T_lo.rearrange("p c t -> p (c t)"), xpose[:],
                                    x3T_hi.rearrange("p c t -> p (c t)"), ALU.subtract).then_inc(normT_lo_ready, 1)
            for f in range(NF + 1):
                if f < NF:
                    n = 256 * groups[f]
                    dve.wait_ge(silu_ready, f + 1)
                    dve.wait_ge(up_ready, f + 1)
                    c = groups[f]
                    for k in range(c):
                        last = nc.vector.tensor_tensor(chunked(h_sb[f][:, 0:n], c)[:, k],
                                                       paired(up_bank[f][:, 0:n], c)[:, k],
                                                       paired(silu_sb[f][:, 0:n], c)[:, k], ALU.mult)
                    last.then_inc(h_ready, 1)
                if f >= 1:
                    n = 256 * groups[f - 1]
                    dve.wait_ge(hT_hi_ready, f)
                    nc.vector.tensor_tensor(hT_lo[:, f - 1, 0:n], hT_bank[f - 1][:, 0:n],
                                            hT_hi[:, f - 1, 0:n].bitcast(F32), ALU.subtract).then_inc(hT_lo_ready, 1)
            dve.wait_ge(down_done, 1)
            nc.vector.tensor_tensor(out_sb, x_out[:], x2_sb, ALU.add).then_inc(result_ready, 1)


_INS = ["x", "ctx_4096", "L0_attn_w_qkv", "L0_attn_w_dense", "L0_ffn_W_gate", "L0_ffn_W_up", "L0_ffn_W_down"]


def kernel(**inputs):
    import numpy as np
    import concourse.bacc as bacc
    from concourse.bass_utils import run_bass_kernel_spmd

    nc = bacc.Bacc("TRN2", target_bir_lowering=False, num_devices=1)
    arrays, args = {}, []
    for name in _INS:
        a = np.ascontiguousarray(inputs[name])
        arrays[f"in_{name}"] = a
        args.append(nc.dram_tensor(f"in_{name}", a.shape, mybir.dt.from_np(a.dtype), kind="ExternalInput").ap())
    out = nc.dram_tensor("out", inputs["x"].shape, F32, kind="ExternalOutput").ap()
    perceiver_layer_kernel(nc, *args, out)
    r = run_bass_kernel_spmd(nc, [arrays], core_ids=[0])
    return r.results[0]["out"]
```

```python
from contextlib import ExitStack

import concourse.bass as bass
from concourse import mybir

ALU = mybir.AluOpType
ACT = mybir.ActivationFunctionType
AX_X = mybir.AxisListType.X
F32 = mybir.dt.float32
F32R = mybir.dt.float32r
F16 = mybir.dt.float16
BF16 = mybir.dt.bfloat16
U32 = mybir.dt.uint32

P = 128
TB = 4
RAW_SLOTS = 6
EARLY_SLOTS = 1
AHEAD = 4
WT_SLOTS = 12
TP_BANKS = 3
TURN_SLOTS = 4
TURN_LEAD, HIGH_LEAD, LOW_LEAD = 5, 4, 4
LOW_SHARE = 3
REFILL = 12
GATE_FROM, UP_FROM, DOWN_UNTIL = 1, 33, 3
GATE_EVERY, UP_EVERY, DOWN_EVERY = 3, 4, 2
ATT_SLOTS = 4
PROBS_BY, VALUES_BY = 3, 1
LEAD = 3
EPS = 1e-5
MASKED = -1e30


def plan_blocks(n_ctx, n_kv, n_q):
    blocks = [("ctx", i) for i in range(n_ctx)]
    others = [(kind, i) for i in range(n_kv) for kind in "kv"]
    assert len(others) == AHEAD
    for g in range(AHEAD):
        blocks += [others[g], ("q", g)]
    for g in range(AHEAD, n_q):
        blocks += [("dense", g - AHEAD), ("q", g)]
    return blocks + [("dense", g) for g in range(n_q - AHEAD, n_q)]


def perceiver_layer_kernel(nc: bass.Bass, x, ctx_in, w_qkv, w_dense, w_gate, w_up, w_down, out):
    _, S, D = x.shape
    SK = ctx_in.shape[1]
    HD = w_dense.shape[1]
    M = w_gate.shape[0]
    DH = 128
    KVD = (w_qkv.shape[0] - HD) // 2
    KVH = KVD // DH
    G = HD // KVD
    BW = TB * P
    assert S == P and D == BW and G == TB and SK % BW == 0 and M % (4 * 64) == 0
    SCALE = float(DH) ** -0.5
    NCTX, NKV, NQ = SK // BW, KVD // BW, HD // BW

    BLOCKS = plan_blocks(NCTX, NKV, NQ)
    NB = len(BLOCKS)
    EARLY_BLOCKS = RAW_SLOTS + EARLY_SLOTS
    NU = NB * TB
    last_unit = {k: b * TB + TB - 1 for b, k in enumerate(BLOCKS)}

    by_dve = [BLOCKS[u // TB][0] in "kvq" for u in range(NU)]
    nth = [sum(by_dve[:u]) if by_dve[u] else u - sum(by_dve[:u]) for u in range(NU)]
    tp_units = [u for u in range(NU) if not by_dve[u]]
    turned_units = [u for u in range(NU) if by_dve[u]]
    shared = [by_dve[u] and u < last_unit["dense", 0] and nth[u] % LOW_SHARE == 0 for u in range(NU)]
    nth_low = [sum(shared[:u]) if shared[u] else nth[u] - by_dve[u] * sum(shared[:u]) for u in range(NU)]

    PC_IN = D // 4 // 64
    PC_DN = M // 4 // 64
    JG, JD = M // 32, D // 32
    NF = -(-PC_DN // 2)

    with ExitStack() as ctx:
        def sb(name, shape, dt=F32):
            return ctx.enter_context(nc.sbuf_tensor(name, shape, dt))

        def sem(name):
            return ctx.enter_context(nc.semaphore(name))

        raw = sb("raw", [P, RAW_SLOTS, TB, BW])
        wt_hi = sb("wt_hi", [P, WT_SLOTS, BW], F32R)
        wt_lo = sb("wt_lo", [P, WT_SLOTS, BW], F32R)
        ffn_wt = sb("ffn_wt", [P, 3, M * 2])
        turned = sb("turned", [P, TURN_SLOTS, BW])
        x_sb = sb("x_sb", [P, D])
        x1_sb = sb("x1_sb", [P, D])
        xn_sb = sb("xn_sb", [P, D])
        xT_hi = sb("xT_hi", [P, TB, P], F32R)
        xT_lo = sb("xT_lo", [P, TB, P], F32R)
        kT = sb("kT", [P, KVH, P])
        v_hi = sb("v_hi", [P, KVH, P], F32R)
        v_lo = sb("v_lo", [P, KVH, P], F32R)
        qk_sb = sb("qk_sb", [P, BW])
        qT = sb("qT", [P, G * P])
        p_sb = sb("p_sb", [P, G, P])
        pT_hi = sb("pT_hi", [P, G * P], F32R)
        pT_lo = sb("pT_lo", [P, G * P], F32R)
        aT_hi = sb("aT_hi", [P, ATT_SLOTS, G, P], F32R)
        aT_lo = sb("aT_lo", [P, ATT_SLOTS, G, P], F32R)
        ident = sb("ident", [P, P])
        ident_b = sb("ident_b", [P, P], BF16)
        mask = sb("mask", [P, G, P], BF16)
        stats = sb("stats", [P, 3, 2, 6])
        mv = sb("mv", [P, 3, 2])
        rstd = sb("rstd", [P, 3])
        var_eps = sb("var_eps", [P, 3])
        minus_half = sb("minus_half", [P, 1])
        x_max = sb("x_max", [P, NCTX])
        x_negmax = sb("x_negmax", [P, 2])
        x_sum = sb("x_sum", [P, NCTX])
        x_tot = sb("x_tot", [P, 2])
        s_max = sb("s_max", [P, NQ, G])
        s_negmax = sb("s_negmax", [P, NQ, G])
        s_sum = sb("s_sum", [P, NQ, G])
        s_inv = sb("s_inv", [P, NQ, G])

        flat = ffn_wt[:].rearrange("p a b -> p (a b)")
        xp_sb = flat[:, 0:SK].rearrange("p (b n) -> p b n", b=NCTX)
        xpT_sb = flat[:, SK:2 * SK].rearrange("p (b n) -> p b n", b=NCTX)
        early = flat[:, 2 * SK:2 * SK + EARLY_SLOTS * TB * BW].rearrange("p (s t n) -> p s t n", s=EARLY_SLOTS, t=TB)

        def raw_slot(b):
            if b < EARLY_BLOCKS:
                return b, (raw[:, b] if b < RAW_SLOTS else early[:, b - RAW_SLOTS]), None
            if b == NB - 1:
                return raw_slot(NB - 5)[0], raw[:, raw_slot(NB - 5)[0]], NB - 5
            s = (b - EARLY_BLOCKS) % RAW_SLOTS
            return s, raw[:, s], (b - EARLY_BLOCKS if b < EARLY_BLOCKS + RAW_SLOTS else b - RAW_SLOTS)

        def raw_count(b):
            before = raw_slot(b)[2]
            parts = 4 if by_dve[TB * b] else 0 if b == 0 else 1
            return 16 * parts + (0 if before is None else raw_count(before))

        GROW = M * 2
        area = raw[:].rearrange("p s t n -> p (s t n)")
        down_blocks = (NB - 7, NB - 6)
        down_at = raw_slot(down_blocks[0])[0] * TB * BW
        down_raw = area[:, down_at:down_at + GROW]
        x2_sb, out_sb = area[:, 0:D], area[:, D:2 * D]
        x3T_hi, x3T_lo = (area[:, n * D:n * D + D // 2].bitcast(F16).rearrange("p (c t) -> p c t", c=TB)
                          for n in (2, 3))
        silu_sb = [area[:, (4 + f) * D:(5 + f) * D] for f in range(NF)]
        h_sb = [area[:, (8 + f) * D:(9 + f) * D] for f in range(NF)]
        assert 12 * D <= down_at and raw_slot(down_blocks[1])[0] == raw_slot(down_blocks[0])[0] + 1
        assert 2 * PC_DN + 2 * NF <= 2 * WT_SLOTS and 2 * NF <= WT_SLOTS
        down_w = [wt_hi[:, k] if k < WT_SLOTS else wt_lo[:, 2 * NF + k - WT_SLOTS] for k in range(2 * PC_DN)]
        hT_hi, hT_lo = wt_lo[:, 0:NF], wt_lo[:, NF:2 * NF]

        bank = [ctx.enter_context(nc.psum_tensor(f"bank{i}", [P, BW], F32)) for i in range(8)]
        tp = bank[0:TP_BANKS]
        x_scores = bank[3:3 + NCTX]
        norm_bank = [[bank[7], bank[6]], [bank[5], bank[6]], [bank[5], bank[6]]]
        x_half = [bank[7][:, 0:D // 2], bank[3][:, 0:D // 2]]
        scores, xpose, att_out, dense = bank[4:8]

        dense_last = bank[3]

        def proj_bank(n):
            return dense if n % 2 == 0 and n < 2 * NKV + AHEAD else bank[3]

        raw_landed = [sem(f"raw_landed{i}") for i in range(EARLY_BLOCKS)]
        ctx0_landed = [sem(f"ctx0_landed{c}") for c in range(TB)]
        x_landed = sem("x_landed")
        ffn_landed = [sem(f"ffn_landed{i}") for i in range(3)]
        out_stored = sem("out_stored")
        consts_ready = sem("consts_ready")
        unit_transposed = sem("unit_transposed")
        unit_turned = sem("unit_turned")
        hi_ready = sem("hi_ready")
        turned_hi_ready = sem("turned_hi_ready")
        shared_lo_ready = sem("shared_lo_ready")
        lo_ready = sem("lo_ready")
        turned_lo_ready = sem("turned_lo_ready")
        unit_used = sem("unit_used")
        dense_half = sem("dense_half")
        var_ready = sem("var_ready")
        rstd_ready = sem("rstd_ready")
        norm_ready = sem("norm_ready")
        normT_ready = sem("normT_ready")
        xpose_ready = sem("xpose_ready")
        normT_hi_ready = sem("normT_hi_ready")
        normT_lo_ready = sem("normT_lo_ready")
        qkT_ready = sem("qkT_ready")
        x_negmax_ready = sem("x_negmax_ready")
        x_exp_ready = sem("x_exp_ready")
        x_pT_ready = sem("x_pT_ready")
        x_pT_copied = sem("x_pT_copied")
        x_pv_done = sem("x_pv_done")
        qk_copied = sem("qk_copied")
        v_hi_ready = sem("v_hi_ready")
        v_lo_ready = sem("v_lo_ready")
        scored = sem("scored")
        negmax_ready = sem("negmax_ready")
        exp_ready = sem("exp_ready")
        inv_ready = sem("inv_ready")
        probs_ready = sem("probs_ready")
        pT_ready = sem("pT_ready")
        pT_hi_ready = sem("pT_hi_ready")
        pT_lo_ready = sem("pT_lo_ready")
        att_ready = sem("att_ready")
        aT_hi_ready = sem("aT_hi_ready")
        aT_lo_ready = sem("aT_lo_ready")
        dve_done = sem("dve_done")
        ffn_wt_ready = [sem(f"ffn_wt_ready{i}") for i in range(3)]
        gate_ready = sem("gate_ready")
        up_ready = sem("up_ready")
        silu_ready = sem("silu_ready")
        h_ready = sem("h_ready")
        hT_ready = sem("hT_ready")
        hT_hi_ready = sem("hT_hi_ready")
        down_w_ready = sem("down_w_ready")
        hT_lo_ready = sem("hT_lo_ready")
        down_done = sem("down_done")
        result_ready = sem("result_ready")

        def block_src(kind, i):
            if kind == "dense":
                return w_dense[:, i * BW:(i + 1) * BW].rearrange("(t p) n -> p t n", p=P)
            return ctx_in[0][i * BW:(i + 1) * BW].rearrange("(t p) n -> p t n", p=P)

        def wait_lo(eng, u):
            signal = shared_lo_ready if shared[u] else turned_lo_ready if by_dve[u] else lo_ready
            eng.wait_ge(signal, nth_low[u] + 1)

        def quadrant_src(kind, i, q):
            rows = {"q": w_qkv[0:HD], "k": w_qkv[HD:HD + KVD], "v": w_qkv[HD + KVD:]}[kind]
            return rows[i * BW:(i + 1) * BW, q * P:(q + 1) * P].rearrange("(j b) d -> b j d", b=32)

        def wait_block_used(eng, b):
            if by_dve[TB * b]:
                eng.wait_ge(unit_turned, nth[TB * b + TB - 1] + 1)
            else:
                eng.wait_ge(unit_transposed, nth[TB * b + TB - 1] + 1)

        ffn_place = [0, 2, 1]
        ffn_raw = [ffn_wt[:, 2, :], ffn_wt[:, 1, :], down_raw]
        ffn_dram = [w_gate, w_up, w_down]
        ffn_pc = [PC_IN, PC_IN, PC_DN]
        ffn_j = [JG, JG, JD]
        ffn_step_j = [512 // (32 * pc) for pc in ffn_pc]
        ffn_ops = [j // s for j, s in zip(ffn_j, ffn_step_j)]

        PROJ = [k for k in BLOCKS if k[0] in "kvq"]
        QK = [k for k in PROJ if k[0] != "v"]
        COPY, XPOSE, SCORE, EXP, INVERSE, PROBS, VALUES = range(7)
        when = {}
        for k in PROJ:
            when[k, COPY], when[k, XPOSE] = last_unit[k] + 1, last_unit[k] + 2
            if k[0] == "q":
                before = ("q", k[1] - 1)
                if k[1] > 0:
                    when[k, XPOSE] = max(when[k, XPOSE], when[before, SCORE] + 1)
                    when[k, COPY] = max(when[k, COPY], when[before, XPOSE] + 1)
                when[k, SCORE] = when[k, XPOSE] + (3 if k[1] < NQ - 1 else 2)
                if k[1] > 0:
                    when[k, SCORE] = max(when[k, SCORE], when[before, PROBS])
                when[k, EXP] = when[k, SCORE] + 1
                when[k, INVERSE] = when[k, SCORE] + 3
                due_by = last_unit["dense", k[1]] - TB + 1
                when[k, PROBS] = min(when[k, SCORE] + 7, due_by - PROBS_BY)
                when[k, VALUES] = min(when[k, PROBS] + 3, due_by - VALUES_BY)
        X_AHEAD = NCTX * TB + TURN_SLOTS
        PV_AHEAD = NCTX * TB + WT_SLOTS
        STEPS = range(NCTX * TB, NU)
        AFTER_NORM = [0, NCTX]

        def ahead(step, lead):
            return max(step + lead + 1, PV_AHEAD + lead - HIGH_LEAD + (step - STEPS[0]) * REFILL // 16)

        def due(step, stage):
            return [k for k in PROJ if when.get((k, stage)) == step]

        first = STEPS[0]
        ffn_at = {first + GATE_FROM + GATE_EVERY * n: (0, n) for n in range(ffn_ops[0])}
        ffn_at |= {first + UP_FROM + UP_EVERY * n: (1, n) for n in range(ffn_ops[1])}
        ffn_at |= {NU - DOWN_UNTIL - DOWN_EVERY * (ffn_ops[2] - n): (2, n) for n in range(ffn_ops[2])}
        assert len(ffn_at) == sum(ffn_ops)

        groups = [min(2, PC_DN - 2 * f) for f in range(NF)]
        gate_bank = [bank[i] for i in (0, 2, 4, 0)]
        up_bank = [bank[i] for i in (1, 3, 6, 1)]
        hT_bank = [bank[i] for i in (5, 2, 5, 2)]

        block = ctx.enter_context(nc.Block())

        @block.sync
        def _(sp):
            sp.dma_start(x_sb[:], x[0]).then_inc(x_landed, 16)

            def load_ffn(w, i):
                pc = ffn_pc[w]
                dst = ffn_raw[w].bitcast(F16).rearrange("p (j d) -> p j d", j=ffn_j[w])
                src = ffn_dram[w][:, i * pc * 64:(i + 1) * pc * 64].rearrange("(j b) d -> b j d", b=32)
                sp.dma_start(dst[32 * i:32 * i + 32], src).then_inc(ffn_landed[w], 16)

            for b, (kind, i) in enumerate(BLOCKS):
                slot, dst, old = raw_slot(b)
                if b == EARLY_BLOCKS:
                    for q in range(4):
                        load_ffn(0, q)
                if b == EARLY_BLOCKS + NCTX:
                    for past in range(RAW_SLOTS, EARLY_BLOCKS):
                        wait_block_used(sp, past)
                    for q in range(4):
                        load_ffn(1, q)
                if b == NB - 1:
                    for past in down_blocks:
                        wait_block_used(sp, past)
                    for q in range(4):
                        load_ffn(2, q)
                if old is not None and BLOCKS[old][0] == "ctx":
                    sp.wait_ge(x_pv_done, old + 1 if old < NCTX - 1 else NCTX + 1)
                elif old is not None:
                    wait_block_used(sp, old)
                if by_dve[TB * b]:
                    for q in (0, 2, 1, 3):
                        part = dst[32 * q:32 * q + 32].rearrange("p t n -> p (t n)").rearrange("p (j d) -> p j d", d=P)
                        sp.dma_start(part, quadrant_src(kind, i, q)).then_inc(raw_landed[slot], 16)
                    continue
                src = block_src(kind, i)
                if b == 0:
                    for c in range(TB):
                        s = slice(c * P, (c + 1) * P)
                        sp.dma_start(dst[:, :, s], src[:, :, s]).then_inc(ctx0_landed[c], 16)
                else:
                    sp.dma_start(dst, src).then_inc(raw_landed[slot], 16)
            sp.wait_ge(result_ready, 1)
            sp.dma_start(out[0], out_sb).then_inc(out_stored, 16)
            sp.wait_ge(out_stored, 16)

        CONSTS = 7

        @block.gpsimd
        def _(pool):
            def inverse_root(k):
                pool.wait_ge(var_ready, k + 1)
                nc.gpsimd.tensor_tensor(rstd[:, k:k + 1], var_eps[:, k:k + 1], minus_half[:],
                                        ALU.pow).then_inc(rstd_ready, 1)

            nc.gpsimd.memset(minus_half[:], -0.5).then_inc(consts_ready, 1)
            nc.gpsimd.memset(ident[:], 0.0).then_inc(consts_ready, 1)
            nc.gpsimd.memset(ident_b[:], 0.0).then_inc(consts_ready, 1)
            nc.gpsimd.memset(mask[:], 0.0).then_inc(consts_ready, 1)
            pool.wait_ge(consts_ready, 4)
            for m in (ident, ident_b):
                nc.gpsimd.affine_select(out=m[:], in_=m[:], compare_op=ALU.not_equal, fill=1.0, base=0,
                                        pattern=[[-1, P]], channel_multiplier=1).then_inc(consts_ready, 1)
            nc.gpsimd.affine_select(out=mask[:], in_=mask[:], compare_op=ALU.is_ge, fill=MASKED, base=0,
                                    pattern=[[0, G], [-1, P]], channel_multiplier=1).then_inc(consts_ready, 1)
            done = [0]

            def lows_to(n):
                for u in range(done[0], min(n, NU)):
                    if by_dve[u] and not shared[u]:
                        pool.wait_ge(turned_hi_ready, nth[u] + 1)
                        nc.gpsimd.tensor_tensor(wt_lo[:, u % WT_SLOTS, :], turned[:, nth[u] % TURN_SLOTS, :],
                                                wt_hi[:, u % WT_SLOTS, :].bitcast(F32),
                                                ALU.subtract).then_inc(turned_lo_ready, 1)
                done[0] = max(done[0], min(n, NU))

            inverse_root(0)
            lows_to(PV_AHEAD)
            inverse_root(1)
            for step in STEPS:
                lows_to(ahead(step, LOW_LEAD))
                for kind, g in due(step, INVERSE):
                    if kind != "q":
                        continue
                    pool.wait_ge(inv_ready, g + 1)
                    nc.gpsimd.tensor_tensor(p_sb[:], p_sb[:], s_inv[:, g, :].unsqueeze(2).to_broadcast([P, G, P]),
                                            ALU.mult).then_inc(probs_ready, 1)
            inverse_root(2)

        @block.tensor
        def _(pe):
            done = [0]

            def transposes_to(n):
                for u in range(done[0], min(n, NU)):
                    if by_dve[u]:
                        continue
                    b, c = divmod(u, TB)
                    slot, src, _ = raw_slot(b)
                    tp_bank = tp[nth[u] % TP_BANKS]
                    if b == 0:
                        pe.wait_ge(ctx0_landed[c], 16)
                    elif c == 0:
                        pe.wait_ge(raw_landed[slot], raw_count(b))
                    if nth[u] >= TP_BANKS:
                        wait_lo(pe, tp_units[nth[u] - TP_BANKS])
                    for t in range(TB):
                        last = nc.tensor.transpose(tp_bank[:, t * P:(t + 1) * P],
                                                   src[:, t, c * P:(c + 1) * P], ident[:])
                    last.then_inc(unit_transposed, 1)
                done[0] = max(done[0], min(n, NU))

            def transpose4(dst, tile_of, signal):
                for t in range(TB):
                    last = nc.tensor.transpose(dst[:, t * P:(t + 1) * P], tile_of(t), ident[:])
                last.then_inc(signal, 1)

            def transpose_norm(k):
                for n in range(2):
                    pe.wait_ge(norm_ready, 2 * k + n + 1)
                    for t in range(2):
                        last = nc.tensor.transpose(norm_bank[k][n][:, t * P:(t + 1) * P],
                                                   xn_sb[:, (2 * n + t) * P:(2 * n + t + 1) * P], ident[:])
                    last.then_inc(normT_ready, 1)

            def left(n):
                kind, i = PROJ[n]
                if kind == "v":
                    pe.wait_ge(v_lo_ready, i + 1)
                else:
                    pe.wait_ge(qk_copied, QK.index(PROJ[n]) + 1)

            def product(u):
                b, c = divmod(u, TB)
                kind, i = BLOCKS[b]
                first, final = c == 0, c == TB - 1
                if kind == "dense":
                    hi, lo, dst = aT_hi[:, i % ATT_SLOTS, c, :], aT_lo[:, i % ATT_SLOTS, c, :], dense
                    first, final = first and i == 0, final and i == NQ - 1
                    if c == 0:
                        pe.wait_ge(aT_lo_ready, i + 1)
                    if first:
                        left(2 * NKV + AHEAD - 2)
                elif kind == "ctx":
                    hi, lo, dst = xT_hi[:, c, :], xT_lo[:, c, :], x_scores[i]
                else:
                    n = PROJ.index((kind, i))
                    hi, lo, dst = xT_hi[:, c, :], xT_lo[:, c, :], proj_bank(n)
                    if c == 0 and n >= 2:
                        left(n - 1 if proj_bank(n) is proj_bank(n - 1) else n - 2)
                wait_lo(pe, u)
                w_hi, w_lo = wt_hi[:, u % WT_SLOTS, :], wt_lo[:, u % WT_SLOTS, :]
                if b in AFTER_NORM:
                    k = AFTER_NORM.index(b)
                    pe.wait_ge(normT_hi_ready, 2 * k + c // 2 + 1)
                    nc.tensor.matmul(dst[:], hi, w_hi, start=first, stop=False)
                    nc.tensor.matmul(dst[:], hi, w_lo, start=False, stop=False)
                    if c == TB - 1:
                        for t in range(TB):
                            pe.wait_ge(normT_lo_ready, 2 * k + t // 2 + 1)
                            w_hi = wt_hi[:, (u - c + t) % WT_SLOTS, :]
                            nc.tensor.matmul(dst[:], xT_lo[:, t, :], w_hi, start=False,
                                             stop=(t == TB - 1)).then_inc(unit_used, 1)
                elif b == NB - 1:
                    s = slice(0, BW // 2)
                    nc.tensor.matmul(dst[:, s], hi, w_hi[:, s], start=False, stop=False)
                    nc.tensor.matmul(dst[:, s], hi, w_lo[:, s], start=False, stop=False)
                    mm = nc.tensor.matmul(dst[:, s], lo, w_hi[:, s], start=False, stop=final)
                    if c == TB - 1:
                        mm.then_inc(dense_half, 1)
                        s = slice(BW // 2, BW)
                        for t in range(TB):
                            hi, lo = aT_hi[:, i % ATT_SLOTS, t, :], aT_lo[:, i % ATT_SLOTS, t, :]
                            w_hi, w_lo = wt_hi[:, (u - c + t) % WT_SLOTS, s], wt_lo[:, (u - c + t) % WT_SLOTS, s]
                            nc.tensor.matmul(dense_last[:, s], hi, w_hi, start=(t == 0), stop=False)
                            nc.tensor.matmul(dense_last[:, s], hi, w_lo, start=False, stop=False)
                            nc.tensor.matmul(dense_last[:, s], lo, w_hi, start=False,
                                             stop=(t == TB - 1)).then_inc(unit_used, 1)
                else:
                    nc.tensor.matmul(dst[:], hi, w_hi, start=first, stop=False)
                    nc.tensor.matmul(dst[:], hi, w_lo, start=False, stop=False)
                    nc.tensor.matmul(dst[:], lo, w_hi, start=False, stop=final).then_inc(unit_used, 1)

            pe.wait_ge(consts_ready, CONSTS)
            transposes_to(1)
            transpose_norm(0)

            for u in range(NCTX * TB):
                transposes_to(u + LEAD + 1)
                product(u)

            for b in range(NCTX):
                pe.wait_ge(x_exp_ready, b + 1)
                transpose4(x_scores[b], lambda t: xp_sb[:, b, t * P:(t + 1) * P], x_pT_ready)
            for b in range(NCTX):
                pe.wait_ge(x_pT_copied, b + 1)
                last = b == NCTX - 1
                for n, t in ([(n, t) for n in range(2) for t in range(TB)] if last else
                             [(n, t) for t in range(TB) for n in range(2)]):
                    mm = nc.tensor.matmul(x_half[n], xpT_sb[:, b, t * P:(t + 1) * P],
                                          raw[:, b, t, n * D // 2:(n + 1) * D // 2],
                                          start=(b == 0 and t == 0), stop=(last and t == TB - 1))
                    if t == TB - 1 and (last or n == 1):
                        mm.then_inc(x_pv_done, 1)
            transpose_norm(1)

            transposed = {"qk": 0, "probs": 0}

            def xpose_left():
                if transposed["qk"] > 0:
                    pe.wait_ge(qkT_ready, transposed["qk"])
                if transposed["probs"] > 0:
                    pe.wait_ge(pT_lo_ready, transposed["probs"])

            def transpose_qk(j):
                pe.wait_ge(qk_copied, j + 1)
                xpose_left()
                transposed["qk"] += 1
                transpose4(xpose, lambda t: qk_sb[:, t * P:(t + 1) * P], xpose_ready)

            def score(g):
                pe.wait_ge(qkT_ready, QK.index(("q", g)) + 1)
                if g >= 1:
                    pe.wait_ge(exp_ready, G * g)
                nc.tensor.matmul(scores[:], ident_b[:], mask[:].rearrange("p g t -> p (g t)"),
                                 start=True, stop=False)
                for h in range(G):
                    s = slice(h * P, (h + 1) * P)
                    mm = nc.tensor.matmul(scores[:, s], qT[:, s], kT[:, g, :], start=False, stop=(h == G - 1))
                mm.then_inc(scored, 1)

            def transpose_probs(g):
                pe.wait_ge(probs_ready, g + 1)
                xpose_left()
                transposed["probs"] += 1
                transpose4(xpose, lambda t: p_sb[:, t, :], pT_ready)

            def values(g):
                pe.wait_ge(pT_lo_ready, g + 1)
                if g % TB == 0:
                    pe.wait_ge(v_lo_ready, g // TB + 1)
                if g >= 1:
                    pe.wait_ge(aT_lo_ready, g)
                nc.tensor.matmul(att_out[:], v_hi[:, g, :], pT_hi[:], start=True, stop=False)
                nc.tensor.matmul(att_out[:], v_hi[:, g, :], pT_lo[:], start=False, stop=False)
                nc.tensor.matmul(att_out[:], v_lo[:, g, :], pT_hi[:], start=False, stop=True).then_inc(att_ready, 1)

            for step in STEPS:
                transposes_to(step + LEAD + 1)
                for kind, i in due(step, XPOSE):
                    if kind != "v":
                        transpose_qk(QK.index((kind, i)))
                for kind, i in due(step, SCORE):
                    if kind == "q":
                        score(i)
                for kind, i in due(step, PROBS):
                    if kind == "q":
                        transpose_probs(i)
                for kind, i in due(step, VALUES):
                    if kind == "q":
                        values(i)
                product(step)

            xpose_left()
            transpose_norm(2)

            def gate_up(f):
                n = 64 * groups[f]
                if f == 0:
                    for w in range(2):
                        pe.wait_ge(ffn_wt_ready[w], ffn_ops[w])
                if f == NF - 1:
                    pe.wait_ge(h_ready, 1)
                for w, dst, signal in ((0, gate_bank[f], gate_ready), (1, up_bank[f], up_ready)):
                    view = ffn_wt[:, ffn_place[w], :].bitcast(F16).rearrange("p (c i m h) -> p c i m h", c=PC_IN, i=4, h=2)
                    o = dst[:, 0:4 * n].rearrange("p (i m) -> p i m", i=4)
                    for part in (x3T_hi, x3T_lo):
                        for c in range(TB):
                            if f == 0 and w == 0:
                                pe.wait_ge(normT_hi_ready if part is x3T_hi else normT_lo_ready, 4 + c // 2 + 1)
                            mv_w = view[:, c // 2, :, 128 * f:128 * f + n, c % 2]
                            mm = nc.tensor.matmul(o, part[:, c, :], mv_w, start=(part is x3T_hi and c == 0),
                                                  stop=(part is x3T_lo and c == TB - 1))
                    mm.then_inc(signal, 1)

            def transpose_h(f):
                pe.wait_ge(h_ready, f + 1)
                if f >= 2:
                    pe.wait_ge(hT_lo_ready, f - 1)
                for t in range(2 * groups[f]):
                    last = nc.tensor.transpose(hT_bank[f][:, t * P:(t + 1) * P], h_sb[f][:, t * P:(t + 1) * P], ident[:])
                last.then_inc(hT_ready, 1)

            def down(f):
                pe.wait_ge(hT_lo_ready, f + 1)
                for t in range(2 * groups[f]):
                    k = 4 * f + t
                    pe.wait_ge(down_w_ready, k + 1)
                    nc.tensor.matmul(dense[:], hT_hi[:, f, t * P:(t + 1) * P], down_w[k], start=(k == 0), stop=False)
                    mm = nc.tensor.matmul(dense[:], hT_lo[:, f, t * P:(t + 1) * P], down_w[k], start=False,
                                          stop=(k == 2 * PC_DN - 1))
                if f == NF - 1:
                    mm.then_inc(down_done, 1)

            for f in range(NF + 2):
                if f < NF:
                    gate_up(f)
                if 1 <= f <= NF:
                    transpose_h(f - 1)
                if f >= 2:
                    down(f - 2)

        @block.scalar
        def _(act):
            done = [0]

            def high(u, src, signal):
                if u >= WT_SLOTS:
                    act.wait_ge(unit_used, u - WT_SLOTS + 1)
                nc.scalar.activation(wt_hi[:, u % WT_SLOTS, :], src, ACT.Copy).then_inc(signal, 1)

            def highs_to(n):
                for u in range(done[0], min(n, NU)):
                    if not by_dve[u]:
                        act.wait_ge(unit_transposed, nth[u] + 1)
                        high(u, tp[nth[u] % TP_BANKS][:], hi_ready)
                done[0] = max(done[0], min(n, NU))

            turns_done = [0]

            def turned_highs_to(n):
                for u in range(turns_done[0], min(n, NU)):
                    if by_dve[u]:
                        act.wait_ge(unit_turned, nth[u] + 1)
                        high(u, turned[:, nth[u] % TURN_SLOTS, :], turned_hi_ready)
                turns_done[0] = max(turns_done[0], min(n, NU))

            def norm_high(k, dst):
                for n in range(2):
                    act.wait_ge(normT_ready, 2 * k + n + 1)
                    nc.scalar.activation(dst[:, 2 * n:2 * n + 2, :].rearrange("p c t -> p (c t)"),
                                         norm_bank[k][n][:, 0:2 * P], ACT.Copy).then_inc(normT_hi_ready, 1)

            highs_to(1)
            norm_high(0, xT_hi)
            for u in range(NCTX * TB):
                highs_to(u + LEAD + 1)
            act.wait_ge(x_negmax_ready, 1)
            for b in range(NCTX):
                nc.scalar.activation(xp_sb[:, b, :], x_scores[b][:], ACT.Exp, bias=x_negmax[:, 0:1],
                                     accum_out=x_sum[:, b:b + 1]).then_inc(x_exp_ready, 1)
            turned_highs_to(PV_AHEAD)
            norm_high(1, xT_hi)

            for step in STEPS:
                for kind, i in due(step, COPY):
                    act.wait_ge(unit_used, last_unit[kind, i] + 1)
                    if PROJ[0] == (kind, i):
                        act.wait_ge(rstd_ready, 2)
                    src = proj_bank(PROJ.index((kind, i)))
                    if kind == "v":
                        nc.scalar.activation(v_hi[:, TB * i:TB * i + TB, :].rearrange("p h e -> p (h e)"), src[:],
                                             ACT.Copy, scale=rstd[:, 1:2]).then_inc(v_hi_ready, 1)
                    else:
                        j = QK.index((kind, i))
                        if j >= 1:
                            act.wait_ge(xpose_ready, j)
                        nc.scalar.activation(qk_sb[:], src[:], ACT.Copy, scale=rstd[:, 1:2]).then_inc(qk_copied, 1)
                highs_to(step + LEAD + 1)
                for kind, i in due(step, XPOSE):
                    if kind == "v":
                        continue
                    act.wait_ge(xpose_ready, QK.index((kind, i)) + 1)
                    if kind == "k":
                        dst = kT[:, TB * i:TB * i + TB, :].rearrange("p h t -> p (h t)")
                    else:
                        dst = qT[:]
                        if i >= 1:
                            act.wait_ge(scored, i)
                    nc.scalar.activation(dst, xpose[:], ACT.Copy).then_inc(qkT_ready, 1)
                for kind, i in due(step, EXP):
                    if kind != "q":
                        continue
                    act.wait_ge(negmax_ready, i + 1)
                    if i >= 1:
                        act.wait_ge(pT_ready, i)
                    for h in range(G):
                        nc.scalar.activation(p_sb[:, h, :], scores[:, h * P:(h + 1) * P], ACT.Exp,
                                             bias=s_negmax[:, i, h:h + 1], scale=SCALE,
                                             accum_out=s_sum[:, i, h:h + 1]).then_inc(exp_ready, 1)
                for kind, i in due(step, PROBS):
                    if kind != "q":
                        continue
                    act.wait_ge(pT_ready, i + 1)
                    if i >= 1:
                        act.wait_ge(att_ready, i)
                    nc.scalar.activation(pT_hi[:], xpose[:], ACT.Copy).then_inc(pT_hi_ready, 1)
                for kind, i in due(step, VALUES):
                    if kind != "q":
                        continue
                    act.wait_ge(att_ready, i + 1)
                    if i >= ATT_SLOTS:
                        act.wait_ge(unit_used, last_unit["dense", i - ATT_SLOTS] + 1)
                    nc.scalar.activation(aT_hi[:, i % ATT_SLOTS].rearrange("p h t -> p (h t)"), att_out[:],
                                         ACT.Copy).then_inc(aT_hi_ready, 1)
                turned_highs_to(ahead(step, HIGH_LEAD))

            act.wait_ge(unit_transposed, nth[NU - 1] + 1)
            norm_high(2, x3T_hi)

            act.wait_ge(ffn_wt_ready[2], ffn_ops[2])
            view = ffn_wt[:, ffn_place[2], :].bitcast(F16).rearrange("p (c n h) -> p c h n", c=PC_DN, h=2)

            def down_weights(k0, k1):
                for k in range(k0, min(k1, 2 * PC_DN)):
                    nc.scalar.activation(down_w[k], view[:, k // 2, k % 2, :], ACT.Copy).then_inc(down_w_ready, 1)

            down_weights(0, 7)
            for f in range(NF + 1):
                if f < NF:
                    n = 256 * groups[f]
                    act.wait_ge(gate_ready, f + 1)
                    nc.scalar.activation(silu_sb[f][:, 0:n], gate_bank[f][:, 0:n], ACT.Silu).then_inc(silu_ready, 1)
                if f >= 1:
                    n = 256 * groups[f - 1]
                    act.wait_ge(hT_ready, f)
                    nc.scalar.activation(hT_hi[:, f - 1, 0:n], hT_bank[f - 1][:, 0:n], ACT.Copy).then_inc(hT_hi_ready, 1)
                down_weights(7 + 3 * f, 10 + 3 * f)

        @block.vector
        def _(dve):
            chain = [0]

            def link(ins):
                chain[0] += 1
                ins.then_inc(dve_done, 1)
                dve.wait_ge(dve_done, chain[0])

            done = [0]

            turns_done = [0]

            def turns_to(n):
                for u in range(turns_done[0], min(n, NU)):
                    if not by_dve[u]:
                        continue
                    b, c = divmod(u, TB)
                    slot, src, _ = raw_slot(b)
                    if c == 0:
                        dve.wait_ge(raw_landed[slot], raw_count(b))
                    if nth[u] >= TURN_SLOTS:
                        wait_lo(dve, turned_units[nth[u] - TURN_SLOTS])
                    part = src.rearrange("p t n -> p (t n)").rearrange("p (j d) -> p j d", d=P)[:, :, 32 * c:32 * c + 32]
                    nc.vector.transpose(turned[:, nth[u] % TURN_SLOTS, :].rearrange("p (j b) -> p j b", b=32),
                                        part).then_inc(unit_turned, 1)
                turns_done[0] = max(turns_done[0], min(n, NU))

            def low(u, src):
                nc.vector.tensor_tensor(wt_lo[:, u % WT_SLOTS, :], src, wt_hi[:, u % WT_SLOTS, :].bitcast(F32),
                                        ALU.subtract).then_inc(shared_lo_ready if by_dve[u] else lo_ready, 1)

            def lows_to(n):
                for u in range(done[0], min(n, NU)):
                    if not by_dve[u]:
                        dve.wait_ge(hi_ready, nth[u] + 1)
                        low(u, tp[nth[u] % TP_BANKS][:])
                done[0] = max(done[0], min(n, NU))

            shared_done = [0]

            def shared_lows_to(n):
                for u in range(shared_done[0], min(n, NU)):
                    if shared[u]:
                        dve.wait_ge(turned_hi_ready, nth[u] + 1)
                        low(u, turned[:, nth[u] % TURN_SLOTS, :])
                shared_done[0] = max(shared_done[0], min(n, NU))

            def paired(v, c):
                return v.rearrange("p (i c a h) -> p c h i a", i=4, c=c, h=2)

            def chunked(v, c):
                return v.rearrange("p (c h i a) -> p c h i a", c=c, h=2, i=4)

            def half_stats(k, n, src):
                nc.vector.bn_stats(stats[:, k, n, :], src[:, n * D // 2:(n + 1) * D // 2]).then_inc(dve_done, 1)
                chain[0] += 1

            def variance(k):
                dve.wait_ge(dve_done, chain[0])
                link(nc.vector.bn_aggr(mv[:, k, :], stats[:, k, :, :]))
                nc.vector.tensor_scalar(var_eps[:, k:k + 1], mv[:, k, 1:2], EPS, None, ALU.add).then_inc(var_ready, 1)

            def norm(k, src):
                variance(k)
                dve.wait_ge(rstd_ready, k + 1)
                for n in range(2):
                    s = slice(n * D // 2, (n + 1) * D // 2)
                    dst, part = xn_sb[:, s], src[:, s]
                    if k == 2:
                        dst, part = chunked(xn_sb[:], PC_IN)[:, n], paired(src, PC_IN)[:, n]
                    nc.vector.tensor_scalar(dst, part, mv[:, k, 0:1], rstd[:, k:k + 1], ALU.subtract,
                                            ALU.mult).then_inc(norm_ready, 1)

            def norm_low(k, dst, hi):
                for n in range(2):
                    dve.wait_ge(normT_hi_ready, 2 * k + n + 1)
                    h = slice(2 * n, 2 * n + 2)
                    nc.vector.tensor_tensor(dst[:, h, :].rearrange("p c t -> p (c t)"), norm_bank[k][n][:, 0:2 * P],
                                            hi[:, h, :].rearrange("p c t -> p (c t)"),
                                            ALU.subtract).then_inc(normT_lo_ready, 1)

            def ffn_transpose(w, n):
                if n == 0:
                    dve.wait_ge(ffn_landed[w], 64)
                    if w >= 1:
                        dve.wait_ge(ffn_wt_ready[w - 1], ffn_ops[w - 1])
                j0, j1 = n * ffn_step_j[w], (n + 1) * ffn_step_j[w]
                pc = ffn_pc[w]
                src = ffn_raw[w].bitcast(U32)[:, j0 * pc * 32:j1 * pc * 32]
                dst = ffn_wt[:, ffn_place[w], :].bitcast(U32).rearrange("p (c j b) -> p j c b", c=pc, b=32)[:, j0:j1]
                nc.vector.transpose(dst, src.rearrange("p (j c a) -> p j c a", c=pc, a=32)).then_inc(ffn_wt_ready[w], 1)

            dve.wait_ge(x_landed, 16)
            for n in range(2):
                half_stats(0, n, x_sb)
            norm(0, x_sb[:])
            lows_to(1)
            norm_low(0, xT_lo, xT_hi[:].bitcast(F32))
            for u in range(NCTX * TB):
                lows_to(u + LEAD + 1)
                if u % TB == TB - 1:
                    b = u // TB
                    dve.wait_ge(unit_used, u + 1)
                    nc.vector.tensor_reduce(x_max[:, b:b + 1], x_scores[b][:], AX_X, ALU.max).then_inc(dve_done, 1)
                    chain[0] += 1
            dve.wait_ge(dve_done, chain[0])
            link(nc.vector.tensor_reduce(x_negmax[:, 1:2], x_max[:], AX_X, ALU.max))
            nc.vector.tensor_scalar(x_negmax[:, 0:1], x_negmax[:, 1:2], -1.0, None, ALU.mult).then_inc(x_negmax_ready, 1)
            turns_to(X_AHEAD)
            for b in range(NCTX):
                dve.wait_ge(x_pT_ready, b + 1)
                nc.vector.tensor_copy(xpT_sb[:, b, :], x_scores[b][:]).then_inc(x_pT_copied, 1)
            link(nc.vector.tensor_reduce(x_tot[:, 0:1], x_sum[:], AX_X, ALU.add))
            link(nc.vector.reciprocal(x_tot[:, 1:2], x_tot[:, 0:1]))
            for u in range(X_AHEAD, PV_AHEAD):
                shared_lows_to(u - TURN_SLOTS + 1)
                turns_to(u + 1)
            shared_lows_to(PV_AHEAD)
            for n in range(2):
                s = slice(n * D // 2, (n + 1) * D // 2)
                dve.wait_ge(x_pv_done, NCTX + n)
                link(nc.vector.scalar_tensor_tensor(out=x1_sb[:, s], in0=x_half[n], scalar=x_tot[:, 1:2],
                                                    in1=x_sb[:, s], op0=ALU.mult, op1=ALU.add))
                half_stats(1, n, x1_sb)
            dve.wait_ge(dve_done, chain[0])
            link(nc.vector.bn_aggr(mv[:, 1, :], stats[:, 1, :, :]))
            for n in range(2):
                nc.vector.tensor_scalar(xn_sb[:].rearrange("p (c i a) -> p c i a", c=TB, i=4)[:, 2 * n:2 * n + 2],
                                        x1_sb[:].rearrange("p (i c a) -> p c i a", i=4, c=TB)[:, 2 * n:2 * n + 2],
                                        mv[:, 1, 0:1], None, ALU.subtract).then_inc(norm_ready, 1)
            nc.vector.tensor_scalar(var_eps[:, 1:2], mv[:, 1, 1:2], EPS, None, ALU.add).then_inc(var_ready, 1)
            norm_low(1, xT_lo, xT_hi[:].bitcast(F32))

            for step in STEPS:
                lows_to(step + LEAD + 1)
                for kind, i in due(step, COPY):
                    if kind == "v":
                        dve.wait_ge(v_hi_ready, i + 1)
                        s = slice(TB * i, TB * i + TB)
                        nc.vector.scalar_tensor_tensor(
                            out=v_lo[:, s, :].rearrange("p h e -> p (h e)"),
                            in0=proj_bank(PROJ.index((kind, i)))[:], scalar=rstd[:, 1:2],
                            in1=v_hi[:, s, :].rearrange("p h e -> p (h e)").bitcast(F32),
                            op0=ALU.mult, op1=ALU.subtract).then_inc(v_lo_ready, 1)
                for kind, i in due(step, SCORE):
                    if kind != "q":
                        continue
                    dve.wait_ge(scored, i + 1)
                    link(nc.vector.tensor_reduce(s_max[:, i, :], scores[:].rearrange("p (g t) -> p g t", g=G),
                                                 AX_X, ALU.max))
                    nc.vector.tensor_scalar(s_negmax[:, i, :], s_max[:, i, :], -SCALE, None,
                                            ALU.mult).then_inc(negmax_ready, 1)
                if step in ffn_at:
                    ffn_transpose(*ffn_at[step])
                for kind, i in due(step, INVERSE):
                    if kind != "q":
                        continue
                    dve.wait_ge(exp_ready, G * (i + 1))
                    nc.vector.reciprocal(s_inv[:, i, :], s_sum[:, i, :]).then_inc(inv_ready, 1)
                for kind, i in due(step, PROBS):
                    if kind != "q":
                        continue
                    dve.wait_ge(pT_hi_ready, i + 1)
                    nc.vector.tensor_tensor(pT_lo[:], xpose[:], pT_hi[:].bitcast(F32), ALU.subtract)\
                        .then_inc(pT_lo_ready, 1)
                for kind, i in due(step, VALUES):
                    if kind != "q":
                        continue
                    dve.wait_ge(aT_hi_ready, i + 1)
                    nc.vector.tensor_tensor(aT_lo[:, i % ATT_SLOTS].rearrange("p h t -> p (h t)"), att_out[:],
                                            aT_hi[:, i % ATT_SLOTS].rearrange("p h t -> p (h t)").bitcast(F32),
                                            ALU.subtract).then_inc(aT_lo_ready, 1)
                turns_to(ahead(step, TURN_LEAD))
                shared_lows_to(ahead(step, LOW_LEAD))

            s = slice(D // 2, D)
            dve.wait_ge(dense_half, 1)
            nc.vector.tensor_tensor(x2_sb, dense[:], x1_sb[:], ALU.add).then_inc(dve_done, 1)
            chain[0] += 1
            dve.wait_ge(dve_done, chain[0])
            half_stats(2, 0, x2_sb)
            dve.wait_ge(unit_used, NU)
            link(nc.vector.tensor_tensor(x2_sb[:, s], x2_sb[:, s], dense_last[:, s], ALU.add))
            half_stats(2, 1, x2_sb)
            norm(2, x2_sb)
            norm_low(2, x3T_lo, x3T_hi)
            for f in range(NF + 1):
                if f < NF:
                    n = 256 * groups[f]
                    dve.wait_ge(silu_ready, f + 1)
                    dve.wait_ge(up_ready, f + 1)
                    c = groups[f]
                    for k in range(c):
                        last = nc.vector.tensor_tensor(chunked(h_sb[f][:, 0:n], c)[:, k],
                                                       paired(up_bank[f][:, 0:n], c)[:, k],
                                                       paired(silu_sb[f][:, 0:n], c)[:, k], ALU.mult)
                    last.then_inc(h_ready, 1)
                if f >= 1:
                    n = 256 * groups[f - 1]
                    dve.wait_ge(hT_hi_ready, f)
                    nc.vector.tensor_tensor(hT_lo[:, f - 1, 0:n], hT_bank[f - 1][:, 0:n],
                                            hT_hi[:, f - 1, 0:n].bitcast(F32), ALU.subtract).then_inc(hT_lo_ready, 1)
            dve.wait_ge(down_done, 1)
            nc.vector.tensor_tensor(out_sb, dense[:], x2_sb, ALU.add).then_inc(result_ready, 1)


_INS = ["x", "ctx_4096", "L0_attn_w_qkv", "L0_attn_w_dense", "L0_ffn_W_gate", "L0_ffn_W_up", "L0_ffn_W_down"]


def kernel(**inputs):
    import numpy as np
    import concourse.bacc as bacc
    from concourse.bass_utils import run_bass_kernel_spmd

    nc = bacc.Bacc("TRN2", target_bir_lowering=False, num_devices=1)
    arrays, args = {}, []
    for name in _INS:
        a = np.ascontiguousarray(inputs[name])
        arrays[f"in_{name}"] = a
        args.append(nc.dram_tensor(f"in_{name}", a.shape, mybir.dt.from_np(a.dtype), kind="ExternalInput").ap())
    out = nc.dram_tensor("out", inputs["x"].shape, F32, kind="ExternalOutput").ap()
    perceiver_layer_kernel(nc, *args, out)
    r = run_bass_kernel_spmd(nc, [arrays], core_ids=[0])
    return r.results[0]["out"]
```
